# Optimizing a Trainium2 kernel written in Bass

```python
import numpy as np
import jax
import jax.numpy as jnp

def _softmax(x, axis=-1):
    return jax.nn.softmax(x, axis=axis)

def _gelu(x):
    return jax.nn.gelu(x, approximate=True)

def _silu(x):
    return jax.nn.silu(x)

def _sigmoid(x):
    return jax.nn.sigmoid(x)

def _layernorm(x, axis=-1, eps=1e-05):
    m = jnp.mean(x, axis=axis, keepdims=True)
    v = jnp.var(x, axis=axis, keepdims=True)
    return (x - m) / jnp.sqrt(v + eps)

def _scatter_add(tgt, idx, src, axis=0):
    return tgt.at[idx].add(src)

def _segment_sum(src, seg, n):
    return jax.ops.segment_sum(src, seg, n)
kernel_name = 'mk_seq_preln_d1_jaxref_r4_92ee07'

def setup_inputs(seed: int=0):
    np.random.seed(seed)
    _w = jnp.asarray

    def _L0_attn_setup():
        import jax, jax.numpy as jnp
        import numpy as np
        B, L, IN_DIM = (4, 512, 256)
        H, D = (16, 64)
        OUT_DIM = 256
        key = jax.random.key(seed)
        k1, k2, k3 = jax.random.split(key, 3)
        inputs = jax.random.normal(k1, (B, L, IN_DIM), dtype=jnp.float32)
        W_qkv = jax.random.normal(k2, (IN_DIM, 3 * H * D), dtype=jnp.float32) * IN_DIM ** (-0.5)
        W_out = jax.random.normal(k3, (H * D, OUT_DIM), dtype=jnp.float32) * (H * D) ** (-0.5)
        return {'inputs': inputs, 'W_qkv': W_qkv, 'W_out': W_out}
    _L0_attn_in = _L0_attn_setup()

    def _L0_ffn_setup():
        import jax, jax.numpy as jnp
        import numpy as np
        ALPHA = 1.0
        key = jax.random.key(seed)
        ks = jax.random.split(key, 7)
        B, S, IN, OUT = (8, 2048, 256, 256)
        RANK, DDIM, UDIM = (4, 100, 50)
        return {'hidden_states': jax.random.normal(ks[0], (B, S, IN), dtype=jnp.float32), 'W': jax.random.normal(ks[1], (OUT, IN), dtype=jnp.float32) * 0.02, 'b': jax.random.normal(ks[2], (OUT,), dtype=jnp.float32) * 0.02, 'lora_down': jax.random.normal(ks[3], (RANK, DDIM), dtype=jnp.float32) * 0.1, 'lora_up': jax.random.normal(ks[4], (UDIM, RANK), dtype=jnp.float32) * 0.1, 'down_aux': jax.random.normal(ks[5], (DDIM, IN), dtype=jnp.float32) * 0.03, 'up_aux': jax.random.normal(ks[6], (OUT, UDIM), dtype=jnp.float32) * 0.03}
    _L0_ffn_in = _L0_ffn_setup()
    _d = {'L0_attn_inputs': _L0_attn_in['inputs'], 'L0_attn_W_qkv': _L0_attn_in['W_qkv'], 'L0_attn_W_out': _L0_attn_in['W_out'], 'L0_ffn_W': _L0_ffn_in['W'], 'L0_ffn_b': _L0_ffn_in['b'], 'L0_ffn_lora_down': _L0_ffn_in['lora_down'], 'L0_ffn_lora_up': _L0_ffn_in['lora_up'], 'L0_ffn_down_aux': _L0_ffn_in['down_aux'], 'L0_ffn_up_aux': _L0_ffn_in['up_aux']}
    _x0 = _d['L0_attn_inputs']
    _d['L0_attn_inputs'] = jax.random.normal(jax.random.fold_in(jax.random.key(seed), 1), (2, 2048, 256), dtype=_x0.dtype)
    del _x0
    return _d

def reference(L0_attn_inputs, L0_attn_W_qkv, L0_attn_W_out, L0_ffn_W, L0_ffn_b, L0_ffn_lora_down, L0_ffn_lora_up, L0_ffn_down_aux, L0_ffn_up_aux):

    def _L0_attn_ref(inputs, W_qkv, W_out):
        import jax, jax.numpy as jnp
        import numpy as np
        B, L, IN_DIM = (4, 512, 256)
        H, D = (16, 64)
        OUT_DIM = 256
        b, l, _ = inputs.shape
        qkv = inputs @ W_qkv
        q, k, v = jnp.split(qkv, 3, axis=-1)
        q = q.reshape(b, l, H, D)
        k = k.reshape(b, l, H, D)
        v = v.reshape(b, l, H, D)
        score = jnp.einsum('bihd,bjhd->bijh', q, k) / D ** 0.5
        mask = jnp.tril(jnp.ones((l, l), dtype=score.dtype))[None, :, :, None]
        masked_score = score * mask + 1e+30 * (mask - 1.0)
        wmat = jax.nn.softmax(masked_score, axis=2)
        out = jnp.einsum('bijh,bjhd->bihd', wmat, v).reshape(b, l, H * D)
        return out @ W_out

    def _L0_ffn_ref(hidden_states, W, b, lora_down, lora_up, down_aux, up_aux):
        import jax, jax.numpy as jnp
        import numpy as np
        ALPHA = 1.0
        lilora_weight = up_aux @ (lora_up @ (lora_down @ down_aux))
        base = jnp.einsum('bsi,oi->bso', hidden_states, W) + b
        delta = jnp.einsum('bsi,oi->bso', hidden_states, lilora_weight)
        return base + ALPHA * delta
    x = L0_attn_inputs
    x = x + _L0_attn_ref(_layernorm(x, axis=-1), L0_attn_W_qkv, L0_attn_W_out)
    x = x + _L0_ffn_ref(_layernorm(x, axis=-1), L0_ffn_W, L0_ffn_b, L0_ffn_lora_down, L0_ffn_lora_up, L0_ffn_down_aux, L0_ffn_up_aux)
    return x

_drawn_inputs = setup_inputs


def setup_inputs(seed=0):
    import zlib

    import numpy as np

    out = dict(_drawn_inputs(seed))
    spreads = {}
    factors = {'L0_ffn_b': 2.939,
     'L0_ffn_lora_down': 3.004,
     'L0_ffn_lora_up': 3.341,
     'L0_ffn_down_aux': 3.105,
     'L0_ffn_up_aux': 3.089}
    for name, (base, spread) in spreads.items():
        noise = np.random.default_rng([zlib.crc32(name.encode()), seed]).standard_normal(out[name].shape)
        drawn = base * np.exp(spread * noise) if base else spread * noise
        out[name] = jnp.asarray(drawn.astype(out[name].dtype))
    for name, factor in factors.items():
        out[name] = (out[name] * factor).astype(out[name].dtype)
    return out
```

```python
from contextlib import ExitStack

import concourse.bass as bass
from concourse import mybir

P = 128
F32 = mybir.dt.float32
F32R = mybir.dt.float32r
BF16 = mybir.dt.bfloat16
ALU = mybir.AluOpType
ACT = mybir.ActivationFunctionType
AX = mybir.AxisListType

HEADS = 16
TILE = 512
NB = TILE // P
EPS = 1e-5
LOWEST = -3.0e38


def halves(ap):
    return ap.bitcast(F32)


def refined_rstd(nc, dve, chain, at, var_eps, root, rstd, work):
    nc.vector.reciprocal(work, root).then_inc(chain, 1)
    dve.wait_ge(chain, at + 1)
    nc.vector.tensor_tensor(work, work, var_eps, ALU.mult).then_inc(chain, 1)
    dve.wait_ge(chain, at + 2)
    nc.vector.tensor_tensor(work, work, root, ALU.add).then_inc(chain, 1)
    dve.wait_ge(chain, at + 3)
    nc.vector.tensor_scalar(work, work, 0.5, None, ALU.mult).then_inc(chain, 1)
    dve.wait_ge(chain, at + 4)
    nc.vector.reciprocal(rstd, work).then_inc(chain, 1)
    dve.wait_ge(chain, at + 5)


ROOT_LINKS = 5


def wait_apart(eng, sem, value, other, least):
    value = value if isinstance(value, int) else eng.to_reg(value)
    eng.wait_ge(other, least)
    eng.wait_ge(sem, value)


def project_qkv(nc, x, w_qkv, q_t, k_t, v, consts):
    tokens, cin = x.shape
    C = cin // P
    hd = w_qkv.shape[1] // 3
    tiles = tokens // TILE
    QK = 2 * hd // P
    VH = hd // TILE
    GROUPS = QK + NB * VH
    BANKS = 6
    STAGES = 3
    HALF = GROUPS // 2
    assert GROUPS % BANKS == 0 and HALF % STAGES == 0 and tiles % 2 == 0 and BANKS % 2 == 0

    ctx = ExitStack()
    with ctx:
        sb = lambda name, shape, dt=F32: ctx.enter_context(nc.sbuf_tensor("a_" + name, shape, dt))
        sem = lambda name: ctx.enter_context(nc.semaphore("a_" + name))
        w_raw = sb("w_raw", [P, C, 3 * hd])
        w_hi = sb("w_hi", [P, C, 3 * hd], F32R)
        w_lo = sb("w_lo", [P, C, 3 * hd], F32R)
        x_in = [sb(f"x_in{u}", [P, NB, cin]) for u in range(2)]
        x_norm = [sb(f"x_norm{u}", [P, NB, cin]) for u in range(2)]
        stats = [sb(f"stats{u}", [P, NB, 6]) for u in range(2)]
        mean_var = [sb(f"mean_var{u}", [P, NB, 2]) for u in range(2)]
        var_eps = [sb(f"var_eps{u}", [P, NB]) for u in range(2)]
        root = [sb(f"root{u}", [P, NB]) for u in range(2)]
        work = [sb(f"work{u}", [P, NB]) for u in range(2)]
        rstd = [sb(f"rstd{u}", [P, NB]) for u in range(2)]
        xt_hi = [sb(f"xt_hi{u}", [P, C, TILE], F32R) for u in range(2)]
        xt_lo = [sb(f"xt_lo{u}", [P, C, TILE], F32R) for u in range(2)]
        stage = [[sb(f"stage_{e}{i}", [P, TILE]) for i in range(STAGES)] for e in "ad"]
        turned = ctx.enter_context(nc.psum_tensor("a_turned", [P, C, TILE], F32))
        made = ctx.enter_context(nc.psum_tensor("a_made", [P, BANKS, TILE], F32))

        w_loaded = sem("w_loaded")
        w_hi_ready = sem("w_hi_ready")
        w_lo_ready = sem("w_lo_ready")
        x_loaded = [sem(f"x_loaded{u}") for u in range(2)]
        stats_done = sem("stats_done")
        var_ready = sem("var_ready")
        root_ready = sem("root_ready")
        normalised = sem("normalised")
        transposed = sem("transposed")
        xt_hi_ready = sem("xt_hi_ready")
        xt_lo_ready = sem("xt_lo_ready")
        projected = sem("projected")
        emptied = [sem("emptied_a"), sem("emptied_d")]
        stored = [[sem(f"stored_{e}{i}") for i in range(STAGES)] for e in "ad"]

        def sink(T, g):
            if g < QK:
                dst, row = (q_t, g) if g < QK // 2 else (k_t, g - QK // 2)
                return dst[row * P:(row + 1) * P, bass.ds(T * TILE, TILE)]
            nb, half = divmod(g - QK, VH)
            return v[bass.ds(T * TILE + nb * P, P), half * TILE:(half + 1) * TILE]

        with nc.Block() as block:

            @block.sync
            def _(sp):
                x_t = x.rearrange("(t n p) c -> t p n c", p=P, n=NB)
                for u in range(2):
                    sp.dma_start(x_in[u][:], x_t[u]).then_inc(x_loaded[u], 16)
                sp.dma_start(w_raw[:], w_qkv.rearrange("(c p) n -> p c n", p=P)).then_inc(w_loaded, 16)

                def tile(T, u, ahead):
                    for g in range(GROUPS):
                        e, s = g % 2, (g // 2) % STAGES
                        sp.wait_ge(emptied[e], T * HALF + g // 2 + 1 + BANKS // 2)
                        sp.dma_start(sink(T, g), stage[e][s][:]).then_inc(stored[e][s], 16)
                        if ahead and g == 4:
                            sp.wait_ge(normalised, T + 1)
                            rows = x[bass.ds((T + 2) * TILE, TILE), :].rearrange("(n p) c -> p n c", p=P)
                            sp.dma_start(x_in[u][:], rows).then_inc(x_loaded[u], 16)

                with sp.Fori(0, tiles // 2 - 1) as i:
                    for u in range(2):
                        tile(i * 2 + u, u, True)
                for u in range(2):
                    tile(tiles - 2 + u, u, False)
                for e in range(2):
                    for s in range(STAGES):
                        sp.wait_ge(stored[e][s], 16 * (tiles * HALF // STAGES) + 1)

            @block.tensor
            def _(pe):
                pe.sem_inc(projected, 2 * GROUPS)

                def transposes(T, u):
                    pe.wait_ge(normalised, T + 1)
                    for c in range(C):
                        for n in range(NB):
                            last = nc.tensor.transpose(turned[:, c, n * P:(n + 1) * P],
                                                       x_norm[u][:, n, c * P:(c + 1) * P], consts["ident"][:])
                    last.then_inc(transposed, 1)

                def group(T, u, g):
                    pe.wait_ge(emptied[g % 2], T * HALF + g // 2 + 1)
                    out = made[:, g % BANKS, :]
                    k = 0
                    for c in range(C):
                        for a, b in (("hi", "hi"), ("lo", "hi"), ("hi", "lo")):
                            w = (w_hi if a == "hi" else w_lo)
                            xt = (xt_hi if b == "hi" else xt_lo)[u]
                            if g < QK:
                                lhs, rhs = w[:, c, g * P:(g + 1) * P], xt[:, c, :]
                            else:
                                nb, half = divmod(g - QK, VH)
                                lhs = xt[:, c, nb * P:(nb + 1) * P]
                                rhs = w[:, c, 2 * hd + half * TILE:2 * hd + (half + 1) * TILE]
                            last = nc.tensor.matmul(out, lhs, rhs, start=(k == 0), stop=(k == 3 * C - 1))
                            k += 1
                    last.then_inc(projected, 1)

                def tile(T, u, ahead):
                    pe.wait_ge(xt_lo_ready, T + 1)
                    for g in range(GROUPS):
                        group(T, u, g)
                        if ahead and g == 12:
                            transposes(T + 1, 1 - u)

                transposes(0, 0)
                pe.wait_ge(w_hi_ready, 1)
                pe.wait_ge(w_lo_ready, 1)
                with pe.Fori(0, tiles // 2 - 1) as i:
                    for u in range(2):
                        tile(i * 2 + u, u, True)
                tile(tiles - 2, 0, True)
                tile(tiles - 1, 1, False)

            def empty(eng, e, T, g):
                s = (g // 2) % STAGES
                eng.wait_ge(projected, T * GROUPS + g + 1 + 2 * GROUPS)
                eng.wait_ge(stored[e][s], (T * (HALF // STAGES) + (g // 2) // STAGES) * 16 + 1)
                copy = nc.scalar.copy if e == 0 else nc.vector.tensor_copy
                copy(stage[e][s][:], made[:, g % BANKS, :]).then_inc(emptied[e], 1)

            @block.scalar
            def _(act):
                act.sem_inc(emptied[0], BANKS // 2)
                for s in range(STAGES):
                    act.sem_inc(stored[0][s], 1)

                def take_root(T, u):
                    act.wait_ge(var_ready, T + 1)
                    nc.scalar.activation(root[u][:], var_eps[u][:], ACT.Sqrt).then_inc(root_ready, 1)

                def turn(T, u):
                    act.wait_ge(transposed, T + 1)
                    act.wait_ge(projected, (T + 1) * GROUPS)
                    nc.scalar.copy(xt_hi[u][:], turned[:]).then_inc(xt_hi_ready, 1)

                def tile(T, u, ahead):
                    for g in range(0, GROUPS, 2):
                        empty(act, 0, T, g)
                        if ahead and g == 4:
                            take_root(T + 1, 1 - u)
                        if ahead and g == 14:
                            turn(T + 1, 1 - u)

                take_root(0, 0)
                act.wait_ge(transposed, 1)
                nc.scalar.copy(xt_hi[0][:], turned[:]).then_inc(xt_hi_ready, 1)
                act.wait_ge(w_loaded, 16)
                nc.scalar.copy(w_hi[:], w_raw[:]).then_inc(w_hi_ready, 1)
                with act.Fori(0, tiles // 2 - 1) as i:
                    for u in range(2):
                        tile(i * 2 + u, u, True)
                tile(tiles - 2, 0, True)
                tile(tiles - 1, 1, False)

            @block.vector
            def _(dve):
                dve.sem_inc(emptied[1], BANKS // 2)
                for s in range(STAGES):
                    dve.sem_inc(stored[1][s], 1)
                LINKS = 2 + ROOT_LINKS

                def variances(T, u, loads):
                    dve.wait_ge(x_loaded[u], loads * 16)
                    for n in range(NB):
                        last = nc.vector.bn_stats(stats[u][:, n, :], x_in[u][:, n, :])
                    last.then_inc(stats_done, 1)
                    wait_apart(dve, stats_done, T * LINKS + 1, x_loaded[0], 16)
                    for n in range(NB):
                        last = nc.vector.bn_aggr(mean_var[u][:, n, :], stats[u][:, n, :])
                    last.then_inc(stats_done, 1)
                    dve.wait_ge(stats_done, T * LINKS + 2)
                    nc.vector.tensor_scalar(var_eps[u][:], mean_var[u][:, :, 1], EPS, None,
                                            ALU.add).then_inc(var_ready, 1)

                def normalise(T, u):
                    dve.wait_ge(root_ready, T + 1)
                    refined_rstd(nc, dve, stats_done, T * LINKS + 2, var_eps[u][:], root[u][:], rstd[u][:],
                                 work[u][:])
                    for n in range(NB):
                        last = nc.vector.tensor_scalar(x_norm[u][:, n, :], x_in[u][:, n, :], mean_var[u][:, n, 0:1],
                                                       rstd[u][:, n:n + 1], ALU.subtract, ALU.mult)
                    last.then_inc(normalised, 1)

                def turn(T, u):
                    dve.wait_ge(xt_hi_ready, T + 1)
                    nc.vector.tensor_tensor(xt_lo[u][:], turned[:], halves(xt_hi[u][:]),
                                            ALU.subtract).then_inc(xt_lo_ready, 1)

                def tile(T, u, ahead, i):
                    for g in range(1, GROUPS, 2):
                        empty(dve, 1, T, g)
                        if ahead and g == 1:
                            variances(T + 1, 1 - u, i + 1 + u)
                        if ahead and g == 7:
                            normalise(T + 1, 1 - u)
                        if ahead and g == 17:
                            turn(T + 1, 1 - u)

                variances(0, 0, 1)
                normalise(0, 0)
                turn(0, 0)
                dve.wait_ge(w_hi_ready, 1)
                nc.vector.tensor_tensor(w_lo[:], w_raw[:], halves(w_hi[:]), ALU.subtract).then_inc(w_lo_ready, 1)
                with dve.Fori(0, tiles // 2 - 1) as i:
                    for u in range(2):
                        tile(i * 2 + u, u, True, i)
                tile(tiles - 2, 0, True, tiles // 2 - 1)
                tile(tiles - 1, 1, False, tiles // 2 - 1)


def spread_chunks(units, chunks, nb, recip_parts, first=3, margin=4):
    def width(t, j):
        return 2 * (TILE - max(0, j - nb * t) * P)

    def cost(k):
        ib, c = chunks[k]
        return 2 * min(TILE, (ib + 1) * P - c * TILE) + 360

    total = sum(cost(k) for k in range(len(chunks)))
    room = []
    for s, (t, j) in enumerate(units):
        free = 2.1 * width(t, j)
        if j >= nb * t:
            free -= width(t, j) + 180
        if t > 0 and 2 <= j < 2 + recip_parts:
            free -= 6 * TILE // recip_parts + 180
        room.append(max(free, 0) if first <= s < len(units) - margin else 0)
    scale = total / sum(room)
    out, k, have = [], 0, 0.0
    for s in range(len(units)):
        have += room[s] * scale
        mine = []
        while k < len(chunks) and room[s] and len(mine) < 2 and have >= cost(k) * 0.5:
            mine.append(k)
            have -= cost(k)
            k += 1
        out.append(mine)
    while k < len(chunks):
        out[len(units) - margin].append(k)
        k += 1
    return out


def attention(nc, q_t, k_t, v, o_t, batches, scale, consts):
    hd, tokens = q_t.shape
    L = tokens // batches
    D = hd // HEADS
    assert 2 * D == P and batches == 2
    PAIRS = HEADS // 2
    TI = L // TILE
    KB = L // P

    units = [(t, j) for t in range(TI) for j in range(NB * (t + 1))]
    U = len(units)
    off_of = lambda t, j: max(0, j - NB * t) * P
    chunks = [(ib, c) for ib in range(KB) for c in range(ib // NB + 1)]
    CH = len(chunks)
    CMAX = KB // NB
    SPLIT_SLOTS = [(0, 0, 1), (2, 3, 4), (6, 7, 8), (12, 13, 14)]
    Q_DIFF_SLOTS = [2, 5, 9, 15]
    K_DIFF_SLOTS = [1, 4, 12, 16]
    RECIP_PARTS = 2
    slot_chunks = spread_chunks(units, chunks, NB, RECIP_PARTS)
    LAST_CHUNK_SLOT = max(s for s in range(U) if slot_chunks[s])
    DIAG = NB * TI
    POOL_ADDS = sum(NB * t - 1 for t in range(1, TI))
    PR = 4
    assert U % PR == 0 and U % 2 == 0

    ctx = ExitStack()
    with ctx:
        sb = lambda name, shape, dt=F32: ctx.enter_context(nc.sbuf_tensor("b_" + name, shape, dt))
        ps = lambda name, shape: ctx.enter_context(nc.psum_tensor("b_" + name, shape, F32))
        sem = lambda name: ctx.enter_context(nc.semaphore("b_" + name))
        k_hh = [sb(f"k_hh{u}", [P, 2, L], F32R) for u in range(2)]
        k_l1 = [sb(f"k_l1{u}", [P, 2, L], F32R) for u in range(2)]
        q_hl = [sb(f"q_hl{u}", [P, 2, L], F32R) for u in range(2)]
        q_hm = [sb(f"q_hm{u}", [P, 2, L], F32R) for u in range(2)]
        v_in = [sb(f"v_in{u}", [P, KB, P]) for u in range(2)]
        k_raw = [sb(f"k_raw{i}", [P, 2, TILE]) for i in range(2)]
        q_raw = [sb(f"q_raw{i}", [P, 2, TILE]) for i in range(2)]
        probs = [sb(f"probs{i}", [P, 2, TILE]) for i in range(PR)]
        sum_pool = sb("sum_pool", [P, 2, TILE])
        sum_dve = sb("sum_dve", [P, 2, TILE])
        o_raw = [sb(f"o_raw{i}", [P, TILE]) for i in range(2)]
        o_norm = sb("o_norm", [P, TILE])
        recip = sb("recip", [P, TILE])
        part_max = sb("part_max", [P, 2, KB, CMAX])
        neg_max = sb("neg_max", [P, P])
        max_rows = sb("max_rows", [P, P], F32R)
        scores = [ps(f"scores{i}", [P, 2, TILE]) for i in range(2)]
        rowwise = ps("rowwise", [P, 2, TILE])
        o_acc = ps("o_acc", [P, TILE])
        denom = ps("denom", [P, TILE])

        raw_loaded = [sem(f"raw_loaded{i}") for i in range(2)]
        v_loaded = [sem(f"v_loaded{u}") for u in range(2)]
        prepared = sem("prepared")
        split_hi = sem("split_hi")
        split_lo_q = sem("split_lo_q")
        split_lo_k0 = sem("split_lo_k0")
        split_lo_k = sem("split_lo_k")
        chunk_made = sem("chunk_made")
        chunk_reduced = sem("chunk_reduced")
        neg_max_ready = sem("neg_max_ready")
        max_turned = sem("max_turned")
        max_rows_ready = sem("max_rows_ready")
        max_placed = [sem(f"max_placed{u}") for u in range(2)]
        scores_made = sem("scores_made")
        exp_done = sem("exp_done")
        masked = sem("masked")
        pv_done = sem("pv_done")
        pool_added = sem("pool_added")
        dve_added = sem("dve_added")
        denom_made = sem("denom_made")
        o_copied = sem("o_copied")
        recip_ready = sem("recip_ready")
        o_ready = sem("o_ready")
        o_stored = sem("o_stored")

        def lo_counts(m, p):
            k_part = (split_lo_k0, m + 1) if p == 0 else (split_lo_k, m * (TI - 1) + p)
            return k_part, (split_lo_q, m * TI + p + 1)

        def wait_lo(eng, m, p):
            for which, value in lo_counts(m, p):
                eng.wait_ge(which, value)

        def k_diff(eng, vec, done, m, u, p):
            cols = slice(p * TILE, (p + 1) * TILE)
            eng.wait_ge(split_hi, m * (3 * TI) + 3 * p + 1)
            vec.tensor_tensor(k_l1[u][0:D, :, cols], k_raw[p % 2][0:D], halves(k_hh[u][0:D, :, cols]),
                              ALU.subtract).then_inc(done, 1)

        def q_diff(eng, m, u, p):
            cols = slice(p * TILE, (p + 1) * TILE)
            eng.wait_ge(split_hi, m * (3 * TI) + 3 * p + 3)
            nc.vector.tensor_tensor(q_hl[u][D:P, :, cols], q_raw[p % 2][D:P], halves(q_hm[u][D:P, :, cols]),
                                    ALU.subtract).then_inc(split_lo_q, 1)

        def pieces_of(item, p):
            pair, b = item
            cols = slice(b * L + p * TILE, b * L + (p + 1) * TILE)
            for raw, src in ((k_raw, k_t), (q_raw, q_t)):
                rows = src[bass.ds(pair * P, P), cols].rearrange("(h d) t -> d h t", h=2)
                for half in range(2):
                    yield raw[p % 2][half * D:(half + 1) * D, :, :], rows

        with nc.Block() as block:

            @block.sync
            def _(sp):
                def wait_split(m, p):
                    values = [(which, value if isinstance(value, int) else sp.to_reg(value))
                              for which, value in lo_counts(m, p)]
                    sp.wait_ge(o_stored, 1)
                    for which, value in values:
                        sp.wait_ge(which, value)

                def load_piece(item, p):
                    for dst, src in pieces_of(item, p):
                        sp.dma_start(dst, src).then_inc(raw_loaded[p % 2], 16)

                def load_v(item):
                    pair, b = item
                    src = v[b * L:(b + 1) * L, bass.ds(pair * P, P)].rearrange("(j p) c -> p j c", p=P)
                    sp.dma_start(v_in[b][:], src).then_inc(v_loaded[b], 16)

                def store_o(n, item, t):
                    pair, b = item
                    wait_apart(sp, o_ready, n * TI + t + 1 + 2, o_stored, 1)
                    cols = slice(b * L + t * TILE, b * L + (t + 1) * TILE)
                    sp.dma_start(o_t[bass.ds(pair * P, P), cols], o_norm[:]).then_inc(o_stored, 16)

                def place_max(m, u):
                    sp.wait_ge(max_rows_ready, m + 1)
                    sp.dma_start(halves(q_hm[u][D:D + 1, :, :]).rearrange("o h (b i) -> o (h b) i", i=P),
                                 halves(max_rows[0:2 * KB, :])).then_inc(max_placed[u], 16)

                def item(pair, u, following, second):
                    n = pair * 2 + u
                    nxt = (pair + u, 1 - u)
                    if following:
                        for p in range(2, TI):
                            wait_split(n + 1, p - 2)
                            load_piece(nxt, p)
                        wait_apart(sp, pv_done, n * U + 1 + PR, o_stored, 1)
                        load_v(nxt)
                    store_o(n, (pair, u), 0)
                    store_o(n, (pair, u), 1)
                    if second:
                        for p in range(2):
                            wait_split(n + 1, p + 2)
                            load_piece((pair + 1, u), p)
                    store_o(n, (pair, u), 2)
                    if following:
                        place_max(n + 1, 1 - u)
                    store_o(n, (pair, u), 3)

                sp.sem_inc(o_stored, 1)
                load_piece((0, 0), 0)
                load_piece((0, 0), 1)
                for p in range(2, TI):
                    wait_split(0, p - 2)
                    load_piece((0, 0), p)
                load_v((0, 0))
                for p in range(2):
                    wait_split(0, p + 2)
                    load_piece((0, 1), p)
                place_max(0, 0)
                with sp.Fori(0, PAIRS - 1) as pair:
                    item(pair, 0, True, True)
                    item(pair, 1, True, True)
                item(PAIRS - 1, 0, True, False)
                item(PAIRS - 1, 1, False, False)
                sp.wait_ge(o_stored, 16 * TI * 2 * PAIRS + 1)

            @block.tensor
            def _(pe):
                def score_unit(n, u, s, between=lambda: None):
                    t, j = units[s]
                    if s == 0:
                        pe.wait_ge(max_placed[u], (n - u) * 8 + 16)
                    pe.wait_ge(exp_done, n * U + s + 1)
                    lo = t * TILE + off_of(t, j)
                    lo = min(lo, (t + 1) * TILE - 2 * P)
                    hi = (t + 1) * TILE
                    for h in range(2):
                        out = scores[s % 2][:, h, lo - t * TILE:TILE]
                        keys = slice(j * P, (j + 1) * P)
                        nc.tensor.matmul(out, k_hh[u][:, h, keys], q_hl[u][:, h, lo:hi], start=True, stop=False)
                        last = nc.tensor.matmul(out, k_l1[u][0:D + 1, h, keys], q_hm[u][0:D + 1, h, lo:hi],
                                                start=False, stop=True)
                        if h == 0:
                            between()
                    last.then_inc(scores_made, 1)

                def chunk_waits(m, k, h, first):
                    ib, c = chunks[k]
                    if c == 0 and ib % NB == 0 and h == 0:
                        wait_lo(pe, m, ib // NB)
                    if k == 0 and h == 0 and not first:
                        pe.wait_ge(max_rows_ready, m)
                    if k > 0:
                        pe.wait_ge(chunk_reduced, m * 2 * CH + 2 * k + h - 1)

                def chunk(m, u, k, h, first=False):
                    ib, c = chunks[k]
                    chunk_waits(m, k, h, first)
                    width = min(TILE, (ib + 1) * P - c * TILE)
                    wide = max(width, 2 * P)
                    diagonal = c == ib // NB
                    last = nc.tensor.matmul(rowwise[:, h, 0:wide], q_hl[u][:, h, ib * P:(ib + 1) * P],
                                            k_hh[u][:, h, c * TILE:c * TILE + wide],
                                            start=True, stop=not diagonal)
                    if diagonal:
                        last = nc.tensor.matmul(rowwise[:, h, width - P:width], consts["ident_bf"][:],
                                                consts["above"][:], start=False, stop=True)
                    last.then_inc(chunk_made, 1)

                def turn_max(m):
                    pe.wait_ge(neg_max_ready, m + 1)
                    nc.tensor.transpose(rowwise[:, 0, 0:P], neg_max[:], consts["ident"][:]).then_inc(max_turned, 1)

                def pv_unit(n, u, s):
                    t, j = units[s]
                    off = off_of(t, j)
                    if s == 0:
                        pe.wait_ge(v_loaded[u], (n - u) * 8 + 16)
                    if j == 0:
                        pe.wait_ge(o_copied, n * TI + t + 1)
                    if j >= NB * t:
                        pe.wait_ge(masked, n * DIAG + NB * t + (j - NB * t) + 1)
                    else:
                        pe.wait_ge(exp_done, n * U + s + 1 + 2)
                    for h in range(2):
                        last = nc.tensor.matmul(o_acc[h * D:(h + 1) * D, off:], v_in[u][:, j, h * D:(h + 1) * D],
                                                probs[s % PR][:, h, off:], start=(j == 0), stop=(j == NB * t + NB - 1))
                    last.then_inc(pv_done, 1)

                def denominators(n, t):
                    pe.wait_ge(dve_added, n * DIAG + NB * (t + 1) + NB)
                    pe.wait_ge(recip_ready, n * TI + t + 1)
                    for h in range(2):
                        last = nc.tensor.matmul(denom[h * D:(h + 1) * D, :], consts["ones"][:, 0:D],
                                                sum_dve[:, h, :], start=True, stop=True)
                    last.then_inc(denom_made, 1)

                def item(pair, u, following):
                    n = pair * 2 + u
                    for s, (t, j) in enumerate(units):
                        mine = [(k, h) for k in slot_chunks[s] for h in range(2)] if following else []

                        def one_chunk():
                            if mine:
                                k, h = mine.pop(0)
                                chunk(n + 1, 1 - u, k, h)

                        if s + 1 < U:
                            score_unit(n, u, s + 1, one_chunk)
                        elif following:
                            score_unit(n + 1, 1 - u, 0)
                        one_chunk()
                        if following and s == LAST_CHUNK_SLOT + 1:
                            turn_max(n + 1)
                        pv_unit(n, u, s)
                        while mine:
                            one_chunk()
                        if t > 0 and j == 1:
                            denominators(n, t - 1)
                    denominators(n, TI - 1)

                pe.sem_inc(pv_done, PR)
                pe.wait_ge(prepared, 4)
                for k in range(CH):
                    for h in range(2):
                        chunk(0, 0, k, h, first=True)
                turn_max(0)
                score_unit(0, 0, 0)
                with pe.Fori(0, PAIRS - 1) as pair:
                    item(pair, 0, True)
                    item(pair, 1, True)
                item(PAIRS - 1, 0, True)
                item(PAIRS - 1, 1, False)

            @block.scalar
            def _(act):
                def split_copy(m, u, p, which, loads):
                    cols = slice(p * TILE, (p + 1) * TILE)
                    if which == 0:
                        act.wait_ge(raw_loaded[p % 2], loads)
                        nc.scalar.copy(k_hh[u][:, :, cols], k_raw[p % 2][:]).then_inc(split_hi, 1)
                    elif which == 1:
                        nc.scalar.copy(q_hm[u][:, :, cols], q_raw[p % 2][:]).then_inc(split_hi, 1)
                    else:
                        nc.scalar.copy(q_hl[u][0:D, :, cols], q_raw[p % 2][0:D]).then_inc(split_hi, 1)

                def exponentials(n, s):
                    t, j = units[s]
                    off = off_of(t, j)
                    act.wait_ge(scores_made, n * U + s + 1)
                    act.wait_ge(pv_done, n * U + s + 1)
                    tp, jp = units[s - PR]
                    if s < PR or jp >= NB * tp:
                        before = s + DIAG - NB * TI if s < PR else NB * tp + jp - NB * tp + NB
                        act.wait_ge(dve_added, n * DIAG + before + 1)
                    else:
                        adds = sum(NB * q - 1 for q in range(1, tp)) + max(jp, 1)
                        act.wait_ge(pool_added, n * POOL_ADDS + adds + 1)
                    nc.scalar.activation(probs[s % PR][:, :, off:], scores[s % 2][:, :, off:], ACT.Exp,
                                         scale=scale).then_inc(exp_done, 1)

                def copy_o(n, t):
                    slot = [s for s, (a, _) in enumerate(units) if a == t][-1]
                    act.wait_ge(pv_done, n * U + slot + 1 + PR)
                    act.wait_ge(o_ready, n * TI + t + 1)
                    nc.scalar.copy(o_raw[t % 2][:], o_acc[:]).then_inc(o_copied, 1)

                def item(pair, u, following):
                    n = pair * 2 + u
                    for s, (t, j) in enumerate(units):
                        exponentials(n, s)
                        if s == 0 and following:
                            act.wait_ge(scores_made, n * U + 1)
                        if t > 0 and j == 0:
                            copy_o(n, t - 1)
                        if following:
                            for p in range(TI):
                                for which in range(3):
                                    if SPLIT_SLOTS[p][which] == s:
                                        loads = ((n + 1) * (TI // 2) + p // 2 + 1) * 64
                                        split_copy(n + 1, 1 - u, p, which, loads)
                    copy_o(n, TI - 1)

                act.sem_inc(exp_done, 2)
                act.sem_inc(o_copied, 1)
                for p in range(TI):
                    for which in range(3):
                        split_copy(0, 0, p, which, (p // 2 + 1) * 64)
                with act.Fori(0, PAIRS - 1) as pair:
                    item(pair, 0, True)
                    item(pair, 1, True)
                item(PAIRS - 1, 0, True)
                item(PAIRS - 1, 1, False)

            @block.vector
            def _(dve):
                def reduce_chunk(m, k):
                    ib, c = chunks[k]
                    width = min(TILE, (ib + 1) * P - c * TILE)
                    for h in range(2):
                        dve.wait_ge(chunk_made, m * 2 * CH + 2 * k + h + 1)
                        nc.vector.tensor_reduce(part_max[:, h, ib, c:c + 1], rowwise[:, h, 0:width], AX.X,
                                                ALU.max).then_inc(chunk_reduced, 1)

                def finish_max(m):
                    dve.wait_ge(chunk_reduced, (m + 1) * 2 * CH)
                    nc.vector.tensor_reduce(neg_max[:, 0:2 * KB].rearrange("p (h b) -> p h b", h=2), part_max[:],
                                            AX.X, ALU.max, negate=True).then_inc(neg_max_ready, 1)

                def take_rows(m):
                    dve.wait_ge(max_turned, m + 1)
                    nc.vector.tensor_copy(max_rows[:], rowwise[:, 0, 0:P]).then_inc(max_rows_ready, 1)

                def add_unit(n, s):
                    t, j = units[s]
                    d = j - NB * t
                    off = d * P
                    dve.wait_ge(masked, n * DIAG + NB * t + d + 1)
                    if d == 0 and t == 0:
                        nc.vector.tensor_copy(sum_dve[:], probs[s % PR][:]).then_inc(dve_added, 1)
                        return
                    if d == 0:
                        adds = sum(NB * q - 1 for q in range(1, t + 1))
                        dve.wait_ge(pool_added, n * POOL_ADDS + adds + 1)
                        nc.vector.tensor_tensor(sum_dve[:], sum_pool[:], probs[s % PR][:],
                                                ALU.add).then_inc(dve_added, 1)
                        return
                    dve.wait_ge(dve_added, n * DIAG + NB * t + d + NB)
                    nc.vector.tensor_tensor(sum_dve[:, :, off:], sum_dve[:, :, off:], probs[s % PR][:, :, off:],
                                            ALU.add).then_inc(dve_added, 1)

                def reciprocals(n, t, part, parts):
                    if part == 0:
                        dve.wait_ge(denom_made, n * TI + t + 1)
                        dve.wait_ge(o_ready, n * TI + t + 2)
                    cols = slice(part * TILE // parts, (part + 1) * TILE // parts)
                    last = nc.vector.reciprocal(recip[:, cols], denom[:, cols])
                    if part == parts - 1:
                        last.then_inc(recip_ready, 1)

                def item(pair, u, following):
                    n = pair * 2 + u
                    for s, (t, j) in enumerate(units):
                        if following:
                            for k in slot_chunks[s]:
                                reduce_chunk(n + 1, k)
                            if s == LAST_CHUNK_SLOT:
                                finish_max(n + 1)
                            if s == LAST_CHUNK_SLOT + 1:
                                take_rows(n + 1)
                        if j >= NB * t:
                            add_unit(n, s)
                        if following:
                            if K_DIFF_SLOTS[0] == s:
                                k_diff(dve, nc.vector, split_lo_k0, n + 1, 1 - u, 0)
                            for p in range(TI):
                                if Q_DIFF_SLOTS[p] == s:
                                    q_diff(dve, n + 1, 1 - u, p)
                        if t > 0 and 2 <= j < 2 + RECIP_PARTS:
                            reciprocals(n, t - 1, j - 2, RECIP_PARTS)
                    reciprocals(n, TI - 1, 0, 1)

                dve.sem_inc(dve_added, NB)
                dve.sem_inc(recip_ready, 1)
                for u in range(2):
                    nc.vector.memset(halves(k_l1[u][D:D + 1]), 1.0).then_inc(prepared, 1)
                nc.vector.memset(part_max[:], LOWEST).then_inc(prepared, 1)
                nc.vector.memset(neg_max[:], 0.0).then_inc(prepared, 1)
                dve.wait_ge(prepared, 4)
                k_diff(dve, nc.vector, split_lo_k0, 0, 0, 0)
                for p in range(TI):
                    q_diff(dve, 0, 0, p)
                for k in range(CH):
                    reduce_chunk(0, k)
                finish_max(0)
                take_rows(0)
                with dve.Fori(0, PAIRS - 1) as pair:
                    item(pair, 0, True)
                    item(pair, 1, True)
                item(PAIRS - 1, 0, True)
                item(PAIRS - 1, 1, False)

            @block.gpsimd
            def _(pool):
                def normalise(n, t):
                    pool.wait_ge(recip_ready, n * TI + t + 2)
                    pool.wait_ge(o_copied, n * TI + t + 2)
                    pool.wait_ge(o_stored, (n * TI + t) * 16 + 1)
                    nc.gpsimd.tensor_tensor(o_norm[:], o_raw[t % 2][:], recip[:], ALU.mult).then_inc(o_ready, 1)

                def item(pair, u, following):
                    n = pair * 2 + u
                    adds = 0
                    for s, (t, j) in enumerate(units):
                        if j >= NB * t:
                            off = off_of(t, j)
                            wait_apart(pool, exp_done, n * U + s + 1 + 2, exp_done, 2)
                            block_ = probs[s % PR][:, :, off:off + P]
                            nc.gpsimd.affine_select(out=block_, in_=block_, compare_op=ALU.is_ge, fill=0.0, base=0,
                                                    pattern=[[0, 2], [1, P]], channel_multiplier=-1
                                                    ).then_inc(masked, 1)
                        elif j >= 1:
                            pool.wait_ge(exp_done, n * U + s + 1 + 2)
                            if j == 1:
                                pool.wait_ge(dve_added, n * DIAG + NB * (t - 1) + 1 + NB)
                                first = probs[(s - 1) % PR][:]
                            else:
                                pool.wait_ge(pool_added, n * POOL_ADDS + adds + 1)
                                first = sum_pool[:]
                            nc.gpsimd.tensor_tensor(sum_pool[:], first, probs[s % PR][:], ALU.add
                                                    ).then_inc(pool_added, 1)
                            adds += 1
                        if t > 0 and j == 2 + RECIP_PARTS:
                            normalise(n, t - 1)
                        if following:
                            for p in range(1, TI):
                                if K_DIFF_SLOTS[p] == s:
                                    k_diff(pool, nc.gpsimd, split_lo_k, n + 1, 1 - u, p)
                    normalise(n, TI - 1)

                pool.sem_inc(pool_added, 1)
                pool.sem_inc(o_ready, 2)
                for p in range(1, TI):
                    k_diff(pool, nc.gpsimd, split_lo_k, 0, 0, p)
                with pool.Fori(0, PAIRS - 1) as pair:
                    item(pair, 0, True)
                    item(pair, 1, True)
                item(PAIRS - 1, 0, True)
                item(PAIRS - 1, 1, False)


def project_and_ffn(nc, x, o_t, w_out, bias, out, consts):
    tokens, cin = x.shape
    hd = o_t.shape[0]
    KC = hd // P
    C = cin // P
    tiles = tokens // TILE
    ctx = ExitStack()
    with ctx:
        sb = lambda name, shape, dt=F32: ctx.enter_context(nc.sbuf_tensor("c_" + name, shape, dt))
        sem = lambda name: ctx.enter_context(nc.semaphore("c_" + name))
        wo_raw = sb("wo_raw", [P, KC, cin])
        wo_hi = sb("wo_hi", [P, KC, cin], F32R)
        wo_lo = sb("wo_lo", [P, KC, cin], F32R)
        bias_rows = sb("bias_rows", [P, cin])
        o_in = [sb(f"o_in{u}", [P, KC, TILE]) for u in range(2)]
        o_hi = [sb(f"o_hi{u}", [P, KC, TILE], F32R) for u in range(2)]
        o_lo = [sb(f"o_lo{u}", [P, KC, TILE], F32R) for u in range(2)]
        x_in = [sb(f"x_in{u}", [P, NB, cin]) for u in range(2)]
        x1 = [sb(f"x1{u}", [P, NB, cin]) for u in range(2)]
        x1b = [sb(f"x1b{u}", [P, NB, cin]) for u in range(2)]
        x_norm = [sb(f"x_norm{u}", [P, NB, cin]) for u in range(2)]
        out_sb = [sb(f"out_sb{u}", [P, NB, cin]) for u in range(2)]
        stats = [sb(f"stats{u}", [P, NB, 6]) for u in range(2)]
        mean_var = [sb(f"mean_var{u}", [P, NB, 2]) for u in range(2)]
        var_eps = [sb(f"var_eps{u}", [P, NB]) for u in range(2)]
        root = [sb(f"root{u}", [P, NB]) for u in range(2)]
        work = [sb(f"work{u}", [P, NB]) for u in range(2)]
        rstd = [sb(f"rstd{u}", [P, NB]) for u in range(2)]
        xt = [sb(f"xt{u}", [P, C, TILE]) for u in range(2)]
        y = [ctx.enter_context(nc.psum_tensor(f"c_y{u}", [P, NB, cin], F32)) for u in range(2)]
        turned = ctx.enter_context(nc.psum_tensor("c_turned", [P, C, TILE], F32))
        ffn = ctx.enter_context(nc.psum_tensor("c_ffn", [P, NB, cin], F32))

        w_loaded = sem("w_loaded")
        b_loaded = sem("b_loaded")
        w_hi_ready = sem("w_hi_ready")
        w_lo_ready = sem("w_lo_ready")
        o_loaded = [sem(f"o_loaded{u}") for u in range(2)]
        x_loaded = [sem(f"x_loaded{u}") for u in range(2)]
        o_hi_ready = sem("o_hi_ready")
        o_lo_ready = sem("o_lo_ready")
        y_made = sem("y_made")
        x1_ready = sem("x1_ready")
        chain = sem("chain")
        var_ready = sem("var_ready")
        root_ready = sem("root_ready")
        normalised = sem("normalised")
        transposed = sem("transposed")
        xt_ready = sem("xt_ready")
        ffn_made = sem("ffn_made")
        biased = sem("biased")
        out_ready = sem("out_ready")
        stored = [sem(f"stored{u}") for u in range(2)]
        halfway = tiles // 2

        with nc.Block() as block:

            @block.sync
            def _(sp):
                def load(T, u):
                    sp.dma_start(o_in[u][:], o_t[:, bass.ds(T * TILE, TILE)].rearrange("(k p) t -> p k t", p=P)
                                 ).then_inc(o_loaded[u], 16)
                    sp.dma_start(x_in[u][:], x[bass.ds(T * TILE, TILE), :].rearrange("(n p) c -> p n c", p=P)
                                 ).then_inc(x_loaded[u], 16)

                def store(T, u):
                    sp.wait_ge(out_ready, T + 1 + 2)
                    sp.dma_start(out[bass.ds(T * TILE, TILE), :].rearrange("(n p) c -> p n c", p=P), out_sb[u][:]
                                 ).then_inc(stored[u], 16)

                for u in range(2):
                    sp.sem_inc(stored[u], 1)
                sp.dma_start(wo_raw[:], w_out.rearrange("(k p) n -> p k n", p=P)).then_inc(w_loaded, 16)
                for u in range(2):
                    load(u, u)
                sp.dma_start(bias_rows[:], bias.rearrange("(o n) -> o n", o=1).broadcast_to([P, cin])).then_inc(b_loaded, 16)
                with sp.Fori(0, halfway - 1) as i:
                    for u in range(2):
                        T = i * 2 + u
                        wait_apart(sp, o_lo_ready, T + 1, w_loaded, 16)
                        sp.wait_ge(x1_ready, T + 1 + 2)
                        load(T + 2, u)
                        store(T, u)
                for u in range(2):
                    store(tiles - 2 + u, u)
                for u in range(2):
                    sp.wait_ge(stored[u], 16 * halfway + 1)

            @block.tensor
            def _(pe):
                def out_project(T, u, blocks):
                    if blocks[0] == 0:
                        pe.wait_ge(o_lo_ready, T + 1)
                        pe.wait_ge(x1_ready, T + 1)
                    for n in blocks:
                        k = 0
                        for kc in range(KC):
                            for a, b in ((o_hi, wo_hi), (o_lo, wo_hi), (o_hi, wo_lo)):
                                last = nc.tensor.matmul(y[u][:, n, :], a[u][:, kc, n * P:(n + 1) * P], b[:, kc, :],
                                                        start=(k == 0), stop=(k == 3 * KC - 1))
                                k += 1
                    if blocks[-1] == NB - 1:
                        last.then_inc(y_made, 1)

                def transposes(T, u):
                    pe.wait_ge(normalised, T + 1)
                    for c in range(C):
                        for n in range(NB):
                            last = nc.tensor.transpose(turned[:, c, n * P:(n + 1) * P],
                                                       x_norm[u][:, n, c * P:(c + 1) * P], consts["ident"][:])
                    last.then_inc(transposed, 1)

                def feed_forward(T, u):
                    pe.wait_ge(xt_ready, T + 1)
                    pe.wait_ge(out_ready, T + 2)
                    for n in range(NB):
                        for c in range(C):
                            last = nc.tensor.matmul(ffn[:, n, :], xt[u][:, c, n * P:(n + 1) * P],
                                                    consts["w_ffn_t"][:, c, :], start=(c == 0), stop=(c == C - 1))
                    last.then_inc(ffn_made, 1)

                def step(T, u):
                    out_project(T, u, [0, 1])
                    transposes(T - 1, 1 - u)
                    out_project(T, u, [2, 3])
                    feed_forward(T - 1, 1 - u)

                pe.wait_ge(w_lo_ready, 1)
                out_project(0, 0, [0, 1, 2, 3])
                with pe.Fori(0, halfway - 1) as i:
                    step(i * 2 + 1, 1)
                    step(i * 2 + 2, 0)
                step(tiles - 1, 1)
                transposes(tiles - 1, 1)
                feed_forward(tiles - 1, 1)

            @block.scalar
            def _(act):
                def high(T, u, loads):
                    act.wait_ge(o_loaded[u], loads * 16)
                    act.wait_ge(y_made, T + 1)
                    nc.scalar.copy(o_hi[u][:], o_in[u][:]).then_inc(o_hi_ready, 1)

                def take_root(T, u):
                    act.wait_ge(var_ready, T + 1)
                    nc.scalar.activation(root[u][:], var_eps[u][:], ACT.Sqrt).then_inc(root_ready, 1)

                def turn(T, u):
                    act.wait_ge(transposed, T + 1)
                    nc.scalar.copy(xt[u][:], turned[:]).then_inc(xt_ready, 1)

                act.sem_inc(y_made, 2)
                act.wait_ge(w_loaded, 16)
                nc.scalar.copy(wo_hi[:], wo_raw[:]).then_inc(w_hi_ready, 1)
                high(0, 0, 1)
                high(1, 1, 1)
                take_root(0, 0)
                with act.Fori(0, halfway - 1) as i:
                    turn(i * 2, 0)
                    high(i * 2 + 2, 0, i + 2)
                    take_root(i * 2 + 1, 1)
                    turn(i * 2 + 1, 1)
                    high(i * 2 + 3, 1, i + 2)
                    take_root(i * 2 + 2, 0)
                turn(tiles - 2, 0)
                take_root(tiles - 1, 1)
                turn(tiles - 1, 1)

            @block.vector
            def _(dve):
                LINKS = 2 + ROOT_LINKS

                def low(T, u):
                    dve.wait_ge(o_hi_ready, T + 1)
                    nc.vector.tensor_tensor(o_lo[u][:], o_in[u][:], halves(o_hi[u][:]),
                                            ALU.subtract).then_inc(o_lo_ready, 1)

                def norm(T, u, loads):
                    dve.wait_ge(x_loaded[u], loads * 16)
                    dve.wait_ge(y_made, T + 1 + 2)
                    dve.wait_ge(biased, T + 1)
                    nc.vector.tensor_tensor(x1[u][:], y[u][:], x_in[u][:], ALU.add).then_inc(x1_ready, 1)
                    dve.wait_ge(x1_ready, T + 1 + 2)
                    for n in range(NB):
                        last = nc.vector.bn_stats(stats[u][:, n, :], x1[u][:, n, :])
                    last.then_inc(chain, 1)
                    wait_apart(dve, chain, T * LINKS + 1, x_loaded[0], 16)
                    for n in range(NB):
                        last = nc.vector.bn_aggr(mean_var[u][:, n, :], stats[u][:, n, :])
                    last.then_inc(chain, 1)
                    dve.wait_ge(chain, T * LINKS + 2)
                    nc.vector.tensor_scalar(var_eps[u][:], mean_var[u][:, :, 1], EPS, None,
                                            ALU.add).then_inc(var_ready, 1)
                    dve.wait_ge(root_ready, T + 1)
                    refined_rstd(nc, dve, chain, T * LINKS + 2, var_eps[u][:], root[u][:], rstd[u][:], work[u][:])
                    for n in range(NB):
                        last = nc.vector.tensor_scalar(x_norm[u][:, n, :], x1[u][:, n, :], mean_var[u][:, n, 0:1],
                                                       rstd[u][:, n:n + 1], ALU.subtract, ALU.mult)
                    last.then_inc(normalised, 1)

                def finish(T, u, uses):
                    dve.wait_ge(ffn_made, T + 1)
                    dve.wait_ge(biased, T + 1 + 2)
                    dve.wait_ge(stored[u], uses * 16 + 1)
                    nc.vector.tensor_tensor(out_sb[u][:], ffn[:], x1b[u][:], ALU.add).then_inc(out_ready, 1)

                dve.sem_inc(x1_ready, 2)
                dve.sem_inc(out_ready, 2)
                dve.wait_ge(w_hi_ready, 1)
                nc.vector.tensor_tensor(wo_lo[:], wo_raw[:], halves(wo_hi[:]), ALU.subtract).then_inc(w_lo_ready, 1)
                low(0, 0)
                low(1, 1)
                norm(0, 0, 1)
                with dve.Fori(0, halfway - 1) as i:
                    low(i * 2 + 2, 0)
                    norm(i * 2 + 1, 1, i + 1)
                    finish(i * 2, 0, i)
                    low(i * 2 + 3, 1)
                    norm(i * 2 + 2, 0, i + 2)
                    finish(i * 2 + 1, 1, i)
                norm(tiles - 1, 1, halfway)
                finish(tiles - 2, 0, halfway - 1)
                finish(tiles - 1, 1, halfway - 1)

            @block.gpsimd
            def _(pool):
                pool.sem_inc(biased, 2)
                pool.wait_ge(b_loaded, 16)
                with pool.Fori(0, halfway) as i:
                    for u in range(2):
                        T = i * 2 + u
                        pool.wait_ge(x1_ready, T + 1 + 2)
                        pool.wait_ge(out_ready, T + 1)
                        for n in range(NB):
                            last = nc.gpsimd.tensor_tensor(x1b[u][:, n, :], x1[u][:, n, :], bias_rows[:], ALU.add)
                        last.then_inc(biased, 1)


def prepare(nc, w_t, down_t, up_t, down_aux, up_aux_t, consts):
    rank = up_t.shape[0]
    ddim, cin = down_aux.shape
    udim = up_t.shape[1]
    C = cin // P
    ctx = ExitStack()
    with ctx:
        sb = lambda name, shape, dt=F32: ctx.enter_context(nc.sbuf_tensor("p_" + name, shape, dt))
        sem = lambda name: ctx.enter_context(nc.semaphore("p_" + name))
        w_in = sb("w_in", [P, C, cin])
        down = sb("down", [ddim, rank])
        aux = sb("aux", [ddim, cin])
        up = sb("up", [rank, udim])
        up_aux = sb("up_aux", [udim, cin])
        d_sb = sb("d_sb", [rank, cin])
        t_sb = sb("t_sb", [udim, cin])
        d_ps = ctx.enter_context(nc.psum_tensor("p_d_ps", [rank, cin], F32))
        t_ps = ctx.enter_context(nc.psum_tensor("p_t_ps", [udim, cin], F32))
        l_ps = ctx.enter_context(nc.psum_tensor("p_l_ps", [P, C, cin], F32))
        loaded = sem("loaded")
        d_made = sem("d_made")
        d_copied = sem("d_copied")
        t_made = sem("t_made")
        t_copied = sem("t_copied")
        l_made = sem("l_made")
        merged = sem("merged")
        filled = sem("filled")

        with nc.Block() as block:

            @block.sync
            def _(sp):
                for dst, src in ((w_in[:], w_t.rearrange("(c p) n -> p c n", p=P)), (down[:], down_t[:, :]),
                                 (aux[:], down_aux[:, :]), (up[:], up_t[:, :]), (up_aux[:], up_aux_t[:, :])):
                    sp.dma_start(dst, src).then_inc(loaded, 16)

            @block.gpsimd
            def _(pool):
                nc.gpsimd.memset(consts["ident"][:], 0.0).then_inc(filled, 1)
                nc.gpsimd.memset(consts["ident_bf"][:], 0.0).then_inc(filled, 1)
                nc.gpsimd.memset(consts["above"][:], 0.0).then_inc(filled, 1)
                nc.gpsimd.memset(consts["ones"][:], 1.0).then_inc(filled, 1)
                pool.wait_ge(filled, 4)
                for name in ("ident", "ident_bf"):
                    nc.gpsimd.affine_select(out=consts[name][:], in_=consts[name][:], compare_op=ALU.not_equal,
                                            fill=1.0, base=0, pattern=[[-1, P]], channel_multiplier=1
                                            ).then_inc(filled, 1)
                nc.gpsimd.affine_select(out=consts["above"][:], in_=consts["above"][:], compare_op=ALU.is_ge,
                                        fill=LOWEST, base=0, pattern=[[-1, P]], channel_multiplier=1
                                        ).then_inc(filled, 1)
                pool.wait_ge(filled, 7)

            @block.tensor
            def _(pe):
                pe.wait_ge(loaded, 16 * 5)
                nc.tensor.matmul(d_ps[:], down[:], aux[:], start=True, stop=True).then_inc(d_made, 1)
                pe.wait_ge(d_copied, 1)
                nc.tensor.matmul(t_ps[:], up[:], d_sb[:], start=True, stop=True).then_inc(t_made, 1)
                pe.wait_ge(t_copied, 1)
                for c in range(C):
                    last = nc.tensor.matmul(l_ps[:, c, :], t_sb[:, c * P:(c + 1) * P], up_aux[:], start=True, stop=True)
                last.then_inc(l_made, 1)

            @block.vector
            def _(dve):
                dve.wait_ge(d_made, 1)
                nc.vector.tensor_copy(d_sb[:], d_ps[:]).then_inc(d_copied, 1)
                dve.wait_ge(t_made, 1)
                nc.vector.tensor_copy(t_sb[:], t_ps[:]).then_inc(t_copied, 1)
                dve.wait_ge(l_made, 1)
                dve.wait_ge(loaded, 16 * 5)
                nc.vector.tensor_tensor(consts["w_ffn_t"][:], l_ps[:], w_in[:], ALU.add).then_inc(merged, 1)
                dve.wait_ge(merged, 1)


def build(nc, x, w_qkv, w_out, w_t, bias, down_t, up_t, down_aux, up_aux_t, out):
    batches, length, cin = x.shape
    tokens = batches * length
    hd = w_qkv.shape[1] // 3
    rows = x.rearrange("b l c -> (b l) c")
    out_rows = out.rearrange("b l c -> (b l) c")
    q_t = nc.dram_tensor("q_t", [hd, tokens], F32).ap()
    k_t = nc.dram_tensor("k_t", [hd, tokens], F32).ap()
    v = nc.dram_tensor("v", [tokens, hd], F32).ap()
    o_t = nc.dram_tensor("o_t", [hd, tokens], F32).ap()
    with ExitStack() as ctx:
        sb = lambda name, shape, dt=F32: ctx.enter_context(nc.sbuf_tensor("p_" + name, shape, dt))
        consts = {
            "ident": sb("ident", [P, P]),
            "ident_bf": sb("ident_bf", [P, P], BF16),
            "above": sb("above", [P, P], BF16),
            "ones": sb("ones", [P, P]),
            "w_ffn_t": sb("w_ffn_t", [P, cin // P, cin]),
        }
        prepare(nc, w_t, down_t, up_t, down_aux, up_aux_t, consts)
        project_qkv(nc, rows, w_qkv, q_t, k_t, v, consts)
        attention(nc, q_t, k_t, v, o_t, batches, float(hd // HEADS) ** -0.5, consts)
        project_and_ffn(nc, rows, o_t, w_out, bias, out_rows, consts)


def kernel(L0_attn_inputs, L0_attn_W_qkv, L0_attn_W_out, L0_ffn_W, L0_ffn_b, L0_ffn_lora_down,
           L0_ffn_lora_up, L0_ffn_down_aux, L0_ffn_up_aux):
    import numpy as np
    import concourse.bacc as bacc
    from concourse.bass_utils import run_bass_kernel_spmd

    given = {
        "x": L0_attn_inputs,
        "w_qkv": L0_attn_W_qkv,
        "w_out": L0_attn_W_out,
        "w_t": np.asarray(L0_ffn_W).T,
        "bias": L0_ffn_b,
        "down_t": np.asarray(L0_ffn_lora_down).T,
        "up_t": np.asarray(L0_ffn_lora_up).T,
        "down_aux": L0_ffn_down_aux,
        "up_aux_t": np.asarray(L0_ffn_up_aux).T,
    }
    nc = bacc.Bacc("TRN2", target_bir_lowering=False, num_devices=1)
    arrays, aps = {}, []
    for name, value in given.items():
        value = np.ascontiguousarray(value)
        arrays[f"in_{name}"] = value
        aps.append(nc.dram_tensor(f"in_{name}", value.shape, mybir.dt.from_np(value.dtype), kind="ExternalInput").ap())
    shape = arrays["in_x"].shape
    out = nc.dram_tensor("out", shape, F32, kind="ExternalOutput").ap()
    build(nc, *aps, out)
    result = run_bass_kernel_spmd(nc, [arrays], core_ids=[0])
    return result.results[0]["out"]
```

```python
from contextlib import ExitStack

import concourse.bass as bass
from concourse import mybir

P = 128
F32 = mybir.dt.float32
F32R = mybir.dt.float32r
BF16 = mybir.dt.bfloat16
ALU = mybir.AluOpType
ACT = mybir.ActivationFunctionType
AX = mybir.AxisListType

HEADS = 16
TILE = 512
NB = TILE // P
EPS = 1e-5
LOWEST = -3.0e38


def halves(ap):
    return ap.bitcast(F32)


def refined_rstd(nc, dve, chain, at, var_eps, root, rstd, work):
    nc.vector.reciprocal(work, root).then_inc(chain, 1)
    dve.wait_ge(chain, at + 1)
    nc.vector.tensor_tensor(work, work, var_eps, ALU.mult).then_inc(chain, 1)
    dve.wait_ge(chain, at + 2)
    nc.vector.tensor_tensor(work, work, root, ALU.add).then_inc(chain, 1)
    dve.wait_ge(chain, at + 3)
    nc.vector.tensor_scalar(work, work, 0.5, None, ALU.mult).then_inc(chain, 1)
    dve.wait_ge(chain, at + 4)
    nc.vector.reciprocal(rstd, work).then_inc(chain, 1)
    dve.wait_ge(chain, at + 5)


ROOT_LINKS = 5


def wait_apart(eng, sem, value, other, least):
    value = value if isinstance(value, int) else eng.to_reg(value)
    eng.wait_ge(other, least)
    eng.wait_ge(sem, value)


def project_qkv(nc, x, w_qkv, q_t, k_t, v, consts):
    tokens, cin = x.shape
    C = cin // P
    hd = w_qkv.shape[1] // 3
    tiles = tokens // TILE
    QK = 2 * hd // P
    VH = hd // TILE
    GROUPS = QK + NB * VH
    BANKS = 6
    STAGES = 3
    W_PARTS = 3 * hd // TILE
    w_cols = lambda p: slice(p * TILE, (p + 1) * TILE)
    HALF = GROUPS // 2
    assert GROUPS % BANKS == 0 and HALF % STAGES == 0 and tiles % 2 == 0 and BANKS % 2 == 0

    ctx = ExitStack()
    with ctx:
        sb = lambda name, shape, dt=F32: ctx.enter_context(nc.sbuf_tensor("a_" + name, shape, dt))
        sem = lambda name: ctx.enter_context(nc.semaphore("a_" + name))
        w_raw = sb("w_raw", [P, C, 3 * hd])
        w_hi = sb("w_hi", [P, C, 3 * hd], F32R)
        w_lo = sb("w_lo", [P, C, 3 * hd], F32R)
        x_in = [sb(f"x_in{u}", [P, NB, cin]) for u in range(2)]
        x_norm = [sb(f"x_norm{u}", [P, NB, cin]) for u in range(2)]
        stats = [sb(f"stats{u}", [P, NB, 6]) for u in range(2)]
        mean_var = [sb(f"mean_var{u}", [P, NB, 2]) for u in range(2)]
        var_eps = [sb(f"var_eps{u}", [P, NB]) for u in range(2)]
        root = [sb(f"root{u}", [P, NB]) for u in range(2)]
        work = [sb(f"work{u}", [P, NB]) for u in range(2)]
        rstd = [sb(f"rstd{u}", [P, NB]) for u in range(2)]
        xt_hi = [sb(f"xt_hi{u}", [P, C, TILE], F32R) for u in range(2)]
        xt_lo = [sb(f"xt_lo{u}", [P, C, TILE], F32R) for u in range(2)]
        stage = [[sb(f"stage_{e}{i}", [P, TILE]) for i in range(STAGES)] for e in "ad"]
        turned = ctx.enter_context(nc.psum_tensor("a_turned", [P, C, TILE], F32))
        made = ctx.enter_context(nc.psum_tensor("a_made", [P, BANKS, TILE], F32))

        w_loaded = [sem(f"w_loaded{p}") for p in range(W_PARTS)]
        w_hi_ready = sem("w_hi_ready")
        w_lo_ready = sem("w_lo_ready")
        x_loaded = [sem(f"x_loaded{u}") for u in range(2)]
        stats_done = sem("stats_done")
        var_ready = sem("var_ready")
        root_ready = sem("root_ready")
        normalised = sem("normalised")
        transposed = sem("transposed")
        xt_hi_ready = sem("xt_hi_ready")
        xt_lo_ready = sem("xt_lo_ready")
        projected = sem("projected")
        emptied = [sem("emptied_a"), sem("emptied_d")]
        stored = [[sem(f"stored_{e}{i}") for i in range(STAGES)] for e in "ad"]

        def sink(T, g):
            if g < QK:
                dst, row = (q_t, g) if g < QK // 2 else (k_t, g - QK // 2)
                return dst[row * P:(row + 1) * P, bass.ds(T * TILE, TILE)]
            nb, half = divmod(g - QK, VH)
            return v[bass.ds(T * TILE + nb * P, P), half * TILE:(half + 1) * TILE]

        with nc.Block() as block:

            @block.sync
            def _(sp):
                x_t = x.rearrange("(t n p) c -> t p n c", p=P, n=NB)
                sp.dma_start(x_in[0][:], x_t[0]).then_inc(x_loaded[0], 16)
                w_rows = w_qkv.rearrange("(c p) n -> p c n", p=P)
                for p in range(W_PARTS):
                    sp.dma_start(w_raw[:, :, w_cols(p)], w_rows[:, :, w_cols(p)]).then_inc(w_loaded[p], 16)
                    if p == 1:
                        sp.dma_start(x_in[1][:], x_t[1]).then_inc(x_loaded[1], 16)

                def tile(T, u, ahead):
                    for g in range(GROUPS):
                        e, s = g % 2, (g // 2) % STAGES
                        sp.wait_ge(emptied[e], T * HALF + g // 2 + 1 + BANKS // 2)
                        sp.dma_start(sink(T, g), stage[e][s][:]).then_inc(stored[e][s], 16)
                        if ahead and g == 4:
                            sp.wait_ge(normalised, T + 1)
                            rows = x[bass.ds((T + 2) * TILE, TILE), :].rearrange("(n p) c -> p n c", p=P)
                            sp.dma_start(x_in[u][:], rows).then_inc(x_loaded[u], 16)

                tile(0, 0, True)
                with sp.Fori(0, tiles // 2 - 2) as i:
                    tile(i * 2 + 1, 1, True)
                    tile(i * 2 + 2, 0, True)
                tile(tiles - 3, 1, True)
                for u in range(2):
                    tile(tiles - 2 + u, u, False)
                for e in range(2):
                    for s in range(STAGES):
                        sp.wait_ge(stored[e][s], 16 * (tiles * HALF // STAGES) + 1)

            @block.tensor
            def _(pe):
                pe.sem_inc(projected, 2 * GROUPS)

                def transposes(T, u):
                    pe.wait_ge(normalised, T + 1)
                    for c in range(C):
                        for n in range(NB):
                            last = nc.tensor.transpose(turned[:, c, n * P:(n + 1) * P],
                                                       x_norm[u][:, n, c * P:(c + 1) * P], consts["ident"][:])
                    last.then_inc(transposed, 1)

                def group(T, u, g, first=False):
                    if first and g % NB == 0 and g <= QK:
                        pe.wait_ge(w_lo_ready, g // NB + 1 if g < QK else W_PARTS)
                    pe.wait_ge(emptied[g % 2], T * HALF + g // 2 + 1)
                    out = made[:, g % BANKS, :]
                    k = 0
                    for c in range(C):
                        for a, b in (("hi", "hi"), ("lo", "hi"), ("hi", "lo")):
                            w = (w_hi if a == "hi" else w_lo)
                            xt = (xt_hi if b == "hi" else xt_lo)[u]
                            if g < QK:
                                lhs, rhs = w[:, c, g * P:(g + 1) * P], xt[:, c, :]
                            else:
                                nb, half = divmod(g - QK, VH)
                                lhs = xt[:, c, nb * P:(nb + 1) * P]
                                rhs = w[:, c, 2 * hd + half * TILE:2 * hd + (half + 1) * TILE]
                            last = nc.tensor.matmul(out, lhs, rhs, start=(k == 0), stop=(k == 3 * C - 1))
                            k += 1
                    last.then_inc(projected, 1)

                def tile(T, u, ahead, first=False):
                    pe.wait_ge(xt_lo_ready, T + 1)
                    for g in range(GROUPS):
                        group(T, u, g, first)
                        if ahead and g == 12:
                            transposes(T + 1, 1 - u)

                transposes(0, 0)
                tile(0, 0, True, True)
                with pe.Fori(0, tiles // 2 - 1) as i:
                    tile(i * 2 + 1, 1, True)
                    tile(i * 2 + 2, 0, True)
                tile(tiles - 1, 1, False)

            def empty(eng, e, T, g):
                s = (g // 2) % STAGES
                eng.wait_ge(projected, T * GROUPS + g + 1 + 2 * GROUPS)
                eng.wait_ge(stored[e][s], (T * (HALF // STAGES) + (g // 2) // STAGES) * 16 + 1)
                copy = nc.scalar.copy if e == 0 else nc.vector.tensor_copy
                copy(stage[e][s][:], made[:, g % BANKS, :]).then_inc(emptied[e], 1)

            @block.scalar
            def _(act):
                act.sem_inc(emptied[0], BANKS // 2)
                for s in range(STAGES):
                    act.sem_inc(stored[0][s], 1)

                def take_root(T, u):
                    act.wait_ge(var_ready, T + 1)
                    nc.scalar.activation(root[u][:], var_eps[u][:], ACT.Sqrt).then_inc(root_ready, 1)

                def turn(T, u):
                    act.wait_ge(transposed, T + 1)
                    act.wait_ge(projected, (T + 1) * GROUPS)
                    nc.scalar.copy(xt_hi[u][:], turned[:]).then_inc(xt_hi_ready, 1)

                def high_part(p):
                    act.wait_ge(w_loaded[p], 16)
                    nc.scalar.copy(w_hi[:, :, w_cols(p)], w_raw[:, :, w_cols(p)]).then_inc(w_hi_ready, 1)

                def tile(T, u, ahead, first=False):
                    for g in range(0, GROUPS, 2):
                        if first and g % 2 == 0 and 2 + g // 2 < W_PARTS:
                            high_part(2 + g // 2)
                        empty(act, 0, T, g)
                        if ahead and g == 4:
                            take_root(T + 1, 1 - u)
                        if ahead and g == 14:
                            turn(T + 1, 1 - u)

                take_root(0, 0)
                act.wait_ge(transposed, 1)
                nc.scalar.copy(xt_hi[0][:], turned[:]).then_inc(xt_hi_ready, 1)
                for p in range(2):
                    high_part(p)
                tile(0, 0, True, True)
                with act.Fori(0, tiles // 2 - 1) as i:
                    tile(i * 2 + 1, 1, True)
                    tile(i * 2 + 2, 0, True)
                tile(tiles - 1, 1, False)

            @block.vector
            def _(dve):
                dve.sem_inc(emptied[1], BANKS // 2)
                for s in range(STAGES):
                    dve.sem_inc(stored[1][s], 1)
                LINKS = 2 + ROOT_LINKS

                def variances(T, u, loads):
                    dve.wait_ge(x_loaded[u], loads * 16)
                    for n in range(NB):
                        last = nc.vector.bn_stats(stats[u][:, n, :], x_in[u][:, n, :])
                    last.then_inc(stats_done, 1)
                    wait_apart(dve, stats_done, T * LINKS + 1, x_loaded[0], 16)
                    for n in range(NB):
                        last = nc.vector.bn_aggr(mean_var[u][:, n, :], stats[u][:, n, :])
                    last.then_inc(stats_done, 1)
                    dve.wait_ge(stats_done, T * LINKS + 2)
                    nc.vector.tensor_scalar(var_eps[u][:], mean_var[u][:, :, 1], EPS, None,
                                            ALU.add).then_inc(var_ready, 1)

                def normalise(T, u):
                    dve.wait_ge(root_ready, T + 1)
                    refined_rstd(nc, dve, stats_done, T * LINKS + 2, var_eps[u][:], root[u][:], rstd[u][:],
                                 work[u][:])
                    for n in range(NB):
                        last = nc.vector.tensor_scalar(x_norm[u][:, n, :], x_in[u][:, n, :], mean_var[u][:, n, 0:1],
                                                       rstd[u][:, n:n + 1], ALU.subtract, ALU.mult)
                    last.then_inc(normalised, 1)

                def turn(T, u):
                    dve.wait_ge(xt_hi_ready, T + 1)
                    nc.vector.tensor_tensor(xt_lo[u][:], turned[:], halves(xt_hi[u][:]),
                                            ALU.subtract).then_inc(xt_lo_ready, 1)

                def low_part(p):
                    dve.wait_ge(w_hi_ready, p + 1)
                    nc.vector.tensor_tensor(w_lo[:, :, w_cols(p)], w_raw[:, :, w_cols(p)],
                                            halves(w_hi[:, :, w_cols(p)]), ALU.subtract).then_inc(w_lo_ready, 1)

                def tile(T, u, ahead, loads, first=False):
                    for g in range(1, GROUPS, 2):
                        if first and 2 + g // 2 < W_PARTS:
                            low_part(2 + g // 2)
                        empty(dve, 1, T, g)
                        if ahead and g == 1:
                            variances(T + 1, 1 - u, loads)
                        if ahead and g == 7:
                            normalise(T + 1, 1 - u)
                        if ahead and g == 17:
                            turn(T + 1, 1 - u)

                variances(0, 0, 1)
                normalise(0, 0)
                turn(0, 0)
                for p in range(2):
                    low_part(p)
                tile(0, 0, True, 1, True)
                with dve.Fori(0, tiles // 2 - 1) as i:
                    tile(i * 2 + 1, 1, True, i + 2)
                    tile(i * 2 + 2, 0, True, i + 2)
                tile(tiles - 1, 1, False, 0)


def spread_chunks(units, chunks, nb, recip_parts, first=3, margin=5):
    def width(t, j):
        return 2 * (TILE - max(0, j - nb * t) * P)

    def cost(k):
        ib, c = chunks[k]
        return 2 * min(TILE, (ib + 1) * P - c * TILE) + 360

    total = sum(cost(k) for k in range(len(chunks)))
    room = []
    for s, (t, j) in enumerate(units):
        free = 2.3 * width(t, j)
        if j >= nb * t:
            free -= width(t, j) + 180
        if 2 <= j < 2 + recip_parts:
            free -= 6 * TILE // recip_parts + 180
        room.append(max(free, 0) if first <= s < len(units) - margin else 0)
    scale = total / sum(room)
    out, k, have = [], 0, 0.0
    for s in range(len(units)):
        have += room[s] * scale
        mine = []
        while k < len(chunks) and room[s] and len(mine) < 2 and have >= cost(k):
            mine.append(k)
            have -= cost(k)
            k += 1
        out.append(mine)
    while k < len(chunks):
        out[len(units) - margin].append(k)
        k += 1
    return out


def attention(nc, q_t, k_t, v, o_t, w_out, batches, scale, consts):
    hd, tokens = q_t.shape
    L = tokens // batches
    D = hd // HEADS
    assert 2 * D == P and batches == 2
    PAIRS = HEADS // 2
    TI = L // TILE
    KB = L // P

    units = [(t, j) for t in range(TI) for j in range(NB * (t + 1))]
    U = len(units)
    off_of = lambda t, j: max(0, j - NB * t) * P
    chunks = [(ib, c) for ib in range(KB) for c in range(ib // NB + 1)]
    CH = len(chunks)
    CMAX = KB // NB
    SPLIT_SLOTS = [(0, 1, 2), (2, 3, 4), (6, 7, 8), (12, 13, 14)]
    Q_DIFF_SLOTS = [2, 5, 9, 15]
    K_DIFF_SLOTS = [1, 4, 12, 16]
    RECIP_PARTS = 3
    slot_chunks = spread_chunks(units, chunks, NB, RECIP_PARTS)
    LAST_CHUNK_SLOT = max(s for s in range(U) if slot_chunks[s])
    DIAG = NB * TI
    LAST_ITEM = 2 * PAIRS - 1
    starts = {NB * t * (t + 1) // 2: t for t in range(TI)}

    def late_tile(n, s, previous):
        t = starts.get(s)
        if t is None or (t == 0 and not previous):
            return []
        return [(n, t - 1)] if t else [(n - 1, TI - 1)]

    POOL_ADDS = sum(NB * t - 1 for t in range(1, TI))
    AHEAD = 2
    PR = 4
    assert U % PR == 0 and U % 2 == 0

    ctx = ExitStack()
    with ctx:
        sb = lambda name, shape, dt=F32: ctx.enter_context(nc.sbuf_tensor("b_" + name, shape, dt))
        ps = lambda name, shape: ctx.enter_context(nc.psum_tensor("b_" + name, shape, F32))
        sem = lambda name: ctx.enter_context(nc.semaphore("b_" + name))
        k_hh = [sb(f"k_hh{u}", [P, 2, L], F32R) for u in range(2)]
        k_l1 = [sb(f"k_l1{u}", [P, 2, L], F32R) for u in range(2)]
        q_hl = [sb(f"q_hl{u}", [P, 2, L], F32R) for u in range(2)]
        q_hm = [sb(f"q_hm{u}", [P, 2, L], F32R) for u in range(2)]
        v_in = [sb(f"v_in{u}", [P, KB, P]) for u in range(2)]
        k_raw = [sb(f"k_raw{i}", [P, 2, TILE]) for i in range(2)]
        q_raw = [sb(f"q_raw{i}", [P, 2, TILE]) for i in range(2)]
        probs = [sb(f"probs{i}", [P, 2, TILE]) for i in range(PR)]
        sum_pool = sb("sum_pool", [P, 2, TILE])
        sum_dve = [sb(f"sum_dve{i}", [P, 2, TILE]) for i in range(2)]
        o_raw = [sb(f"o_raw{i}", [P, TILE]) for i in range(2)]
        o_norm = sb("o_norm", [P, TILE])
        recip = sb("recip", [P, TILE])
        part_max = sb("part_max", [P, 2, KB, CMAX])
        neg_max = sb("neg_max", [P, P])
        max_rows = sb("max_rows", [P, P], F32R)
        scores = [ps(f"scores{i}", [P, 2, TILE]) for i in range(2)]
        rowwise = ps("rowwise", [P, 2, TILE])
        first_buffers = scores + [rowwise]
        o_acc = ps("o_acc", [P, TILE])
        denom = ps("denom", [P, TILE])

        raw_loaded = [sem(f"raw_loaded{i}") for i in range(2)]
        v_loaded = [sem(f"v_loaded{u}") for u in range(2)]
        prepared = sem("prepared")
        ones_placed = sem("ones_placed")
        split_hi = sem("split_hi")
        split_lo_q = sem("split_lo_q")
        split_lo_k0 = sem("split_lo_k0")
        split_lo_k = sem("split_lo_k")
        chunk_made = sem("chunk_made")
        chunk_reduced = sem("chunk_reduced")
        neg_max_ready = sem("neg_max_ready")
        max_turned = sem("max_turned")
        max_rows_ready = sem("max_rows_ready")
        max_placed = [sem(f"max_placed{u}") for u in range(2)]
        scores_made = sem("scores_made")
        exp_done = sem("exp_done")
        masked = sem("masked")
        pv_done = sem("pv_done")
        pool_added = sem("pool_added")
        dve_added = sem("dve_added")
        denom_made = sem("denom_made")
        o_copied = sem("o_copied")
        recip_ready = sem("recip_ready")
        o_ready = sem("o_ready")
        o_stored = sem("o_stored")
        wo_loaded = sem("wo_loaded")

        def lo_counts(m, p):
            k_part = (split_lo_k0, m + 1) if p == 0 else (split_lo_k, m * (TI - 1) + p)
            return k_part, (split_lo_q, m * TI + p + 1)

        def wait_lo(eng, m, p):
            for which, value in lo_counts(m, p):
                eng.wait_ge(which, value)

        def k_diff(eng, vec, done, m, u, p):
            cols = slice(p * TILE, (p + 1) * TILE)
            eng.wait_ge(split_hi, m * (3 * TI) + 3 * p + 1)
            vec.tensor_tensor(k_l1[u][0:D, :, cols], k_raw[p % 2][0:D], halves(k_hh[u][0:D, :, cols]),
                              ALU.subtract).then_inc(done, 1)

        def q_diff(eng, m, u, p):
            cols = slice(p * TILE, (p + 1) * TILE)
            eng.wait_ge(split_hi, m * (3 * TI) + 3 * p + 3)
            nc.vector.tensor_tensor(q_hl[u][D:P, :, cols], q_raw[p % 2][D:P], halves(q_hm[u][D:P, :, cols]),
                                    ALU.subtract).then_inc(split_lo_q, 1)

        def pieces_of(item, p):
            pair, b = item
            cols = slice(b * L + p * TILE, b * L + (p + 1) * TILE)
            for raw, src in ((k_raw, k_t), (q_raw, q_t)):
                rows = src[bass.ds(pair * P, P), cols].rearrange("(h d) t -> d h t", h=2)
                for half in range(2):
                    yield raw[p % 2][half * D:(half + 1) * D, :, :], rows

        with nc.Block() as block:

            @block.sync
            def _(sp):
                def wait_split(m, p):
                    values = [(which, value if isinstance(value, int) else sp.to_reg(value))
                              for which, value in lo_counts(m, p)]
                    sp.wait_ge(o_stored, 1)
                    for which, value in values:
                        sp.wait_ge(which, value)

                def load_piece(item, p):
                    for dst, src in pieces_of(item, p):
                        sp.dma_start(dst, src).then_inc(raw_loaded[p % 2], 16)

                def load_v(item):
                    pair, b = item
                    src = v[b * L:(b + 1) * L, bass.ds(pair * P, P)].rearrange("(j p) c -> p j c", p=P)
                    sp.dma_start(v_in[b][:], src).then_inc(v_loaded[b], 16)

                def store_o(n, item, t):
                    pair, b = item
                    wait_apart(sp, o_ready, n * TI + t + 1 + 2, o_stored, 1)
                    cols = slice(b * L + t * TILE, b * L + (t + 1) * TILE)
                    sp.dma_start(o_t[bass.ds(pair * P, P), cols], o_norm[:]).then_inc(o_stored, 16)

                def place_max(m, u):
                    sp.wait_ge(max_rows_ready, m + 1)
                    sp.dma_start(halves(q_hm[u][D:D + 1, :, :]).rearrange("o h (b i) -> o (h b) i", i=P),
                                 halves(max_rows[0:2 * KB, :])).then_inc(max_placed[u], 16)

                def item(pair, u, following, second, previous=True):
                    n = pair * 2 + u
                    nxt = (pair + u, 1 - u)
                    if following:
                        for p in range(2, TI):
                            wait_split(n + 1, p - 2)
                            load_piece(nxt, p)
                    if previous:
                        store_o(n - 1, (pair - 1 + u, 1 - u), TI - 1)
                    if following:
                        wait_apart(sp, pv_done, n * U + 1 + PR, o_stored, 1)
                        load_v(nxt)
                    store_o(n, (pair, u), 0)
                    store_o(n, (pair, u), 1)
                    if second:
                        for p in range(2):
                            wait_split(n + 1, p + 2)
                            load_piece((pair + 1, u), p)
                    store_o(n, (pair, u), 2)
                    if following:
                        place_max(n + 1, 1 - u)

                sp.sem_inc(o_stored, 1)
                load_piece((0, 0), 0)
                load_piece((0, 0), 1)
                for p in range(2, TI):
                    wait_split(0, p - 2)
                    load_piece((0, 0), p)
                load_v((0, 0))
                for p in range(2):
                    wait_split(0, p + 2)
                    load_piece((0, 1), p)
                place_max(0, 0)
                sp.dma_start(consts["wo_raw"][:], w_out.rearrange("(k p) n -> p k n", p=P)).then_inc(wo_loaded, 16)
                item(0, 0, True, True, False)
                with sp.Fori(0, PAIRS - 2) as pair:
                    item(pair, 1, True, True)
                    item(pair + 1, 0, True, True)
                item(PAIRS - 2, 1, True, True)
                item(PAIRS - 1, 0, True, False)
                item(PAIRS - 1, 1, False, False)
                store_o(2 * PAIRS - 1, (PAIRS - 1, 1), TI - 1)
                sp.wait_ge(o_stored, 16 * TI * 2 * PAIRS + 1)
                sp.wait_ge(wo_loaded, 16)

            @block.tensor
            def _(pe):
                def score_unit(n, u, s, between=lambda: None):
                    t, j = units[s]
                    if s == 0:
                        pe.wait_ge(max_placed[u], (n - u) * 8 + 16)
                    pe.wait_ge(exp_done, n * U + s + 1)
                    lo = t * TILE + off_of(t, j)
                    lo = min(lo, (t + 1) * TILE - 2 * P)
                    hi = (t + 1) * TILE
                    for h in range(2):
                        out = scores[s % 2][:, h, lo - t * TILE:TILE]
                        keys = slice(j * P, (j + 1) * P)
                        nc.tensor.matmul(out, k_hh[u][:, h, keys], q_hl[u][:, h, lo:hi], start=True, stop=False)
                        last = nc.tensor.matmul(out, k_l1[u][0:D + 1, h, keys], q_hm[u][0:D + 1, h, lo:hi],
                                                start=False, stop=True)
                        if h == 0:
                            between()
                    last.then_inc(scores_made, 1)

                def chunk_waits(m, k, h):
                    ib, c = chunks[k]
                    if c == 0 and ib % NB == 0 and h == 0:
                        wait_lo(pe, m, ib // NB)
                    if k == 0 and h == 0:
                        pe.wait_ge(max_rows_ready, m)
                    if k > 0:
                        pe.wait_ge(chunk_reduced, m * 2 * CH + 2 * k + h - 1)

                def chunk(m, u, k, h):
                    chunk_waits(m, k, h)
                    chunk_products(u, k, h, rowwise)

                def chunk_products(u, k, h, rowwise):
                    ib, c = chunks[k]
                    width = min(TILE, (ib + 1) * P - c * TILE)
                    wide = max(width, 2 * P)
                    diagonal = c == ib // NB
                    last = nc.tensor.matmul(rowwise[:, h, 0:wide], q_hl[u][:, h, ib * P:(ib + 1) * P],
                                            k_hh[u][:, h, c * TILE:c * TILE + wide],
                                            start=True, stop=not diagonal)
                    if diagonal:
                        last = nc.tensor.matmul(rowwise[:, h, width - P:width], consts["ident_bf"][:],
                                                consts["above"][:], start=False, stop=True)
                    last.then_inc(chunk_made, 1)

                def turn_max(m):
                    pe.wait_ge(neg_max_ready, m + 1)
                    nc.tensor.transpose(rowwise[:, 0, 0:P], neg_max[:], consts["ident"][:]).then_inc(max_turned, 1)

                def pv_unit(n, u, s):
                    t, j = units[s]
                    off = off_of(t, j)
                    if s == 0:
                        pe.wait_ge(v_loaded[u], (n - u) * 8 + 16)
                    if j == 0:
                        pe.wait_ge(o_copied, n * TI + t + 1)
                    if j >= NB * t:
                        pe.wait_ge(masked, n * DIAG + NB * t + (j - NB * t) + 1)
                    else:
                        pe.wait_ge(exp_done, n * U + s + 1 + 2)
                    for h in range(2):
                        last = nc.tensor.matmul(o_acc[h * D:(h + 1) * D, off:], v_in[u][:, j, h * D:(h + 1) * D],
                                                probs[s % PR][:, h, off:], start=(j == 0), stop=(j == NB * t + NB - 1))
                    last.then_inc(pv_done, 1)

                def denominators(n, t):
                    pe.wait_ge(dve_added, n * DIAG + NB * (t + 1) + NB)
                    pe.wait_ge(recip_ready, n * TI + t + 1)
                    for h in range(2):
                        last = nc.tensor.matmul(denom[h * D:(h + 1) * D, :], consts["ones"][:, 0:D],
                                                sum_dve[t % 2][:, h, :], start=True, stop=True)
                    last.then_inc(denom_made, 1)

                def item(pair, u, following, previous=True):
                    n = pair * 2 + u
                    for s, (t, j) in enumerate(units):
                        mine = [(k, h) for k in slot_chunks[s] for h in range(2)] if following else []

                        def one_chunk():
                            if mine:
                                k, h = mine.pop(0)
                                chunk(n + 1, 1 - u, k, h)

                        if s + AHEAD < U:
                            score_unit(n, u, s + AHEAD, one_chunk)
                        elif following:
                            score_unit(n + 1, 1 - u, s + AHEAD - U)
                        one_chunk()
                        pv_unit(n, u, s)
                        if following and s == LAST_CHUNK_SLOT + 1:
                            turn_max(n + 1)
                        while mine:
                            one_chunk()
                        for late in late_tile(n, s - 1, previous):
                            denominators(*late)

                pe.sem_inc(pv_done, PR)
                for k in range(CH):
                    ib, c = chunks[k]
                    if c == 0 and ib % NB == 0:
                        wait_lo(pe, 0, ib // NB)
                    if k >= 3:
                        pe.wait_ge(chunk_reduced, 2 * (k - 2))
                    for h in range(2):
                        chunk_products(0, k, h, first_buffers[k % 3])
                turn_max(0)
                pe.wait_ge(ones_placed, 2)
                for s in range(AHEAD):
                    score_unit(0, 0, s)
                item(0, 0, True, False)
                with pe.Fori(0, PAIRS - 1) as pair:
                    item(pair, 1, True)
                    item(pair + 1, 0, True)
                item(PAIRS - 1, 1, False)
                denominators(LAST_ITEM, TI - 1)

            @block.scalar
            def _(act):
                def split_copy(m, u, p, which, loads):
                    cols = slice(p * TILE, (p + 1) * TILE)
                    if which == 0:
                        act.wait_ge(raw_loaded[p % 2], loads)
                        nc.scalar.copy(k_hh[u][:, :, cols], k_raw[p % 2][:]).then_inc(split_hi, 1)
                    elif which == 1:
                        nc.scalar.copy(q_hm[u][:, :, cols], q_raw[p % 2][:]).then_inc(split_hi, 1)
                    else:
                        nc.scalar.copy(q_hl[u][0:D, :, cols], q_raw[p % 2][0:D]).then_inc(split_hi, 1)

                def exponentials(n, s):
                    t, j = units[s]
                    off = off_of(t, j)
                    act.wait_ge(scores_made, n * U + s + 1)
                    act.wait_ge(pv_done, n * U + s + 1)
                    tp, jp = units[s - PR]
                    if s < PR or jp >= NB * tp:
                        before = s + DIAG - NB * TI if s < PR else NB * tp + jp - NB * tp + NB
                        act.wait_ge(dve_added, n * DIAG + before + 1)
                    else:
                        adds = sum(NB * q - 1 for q in range(1, tp)) + max(jp, 1)
                        act.wait_ge(pool_added, n * POOL_ADDS + adds + 1)
                    nc.scalar.activation(probs[s % PR][:, :, off:], scores[s % 2][:, :, off:], ACT.Exp,
                                         scale=scale).then_inc(exp_done, 1)

                def copy_o(n, t):
                    slot = [s for s, (a, _) in enumerate(units) if a == t][-1]
                    act.wait_ge(pv_done, n * U + slot + 1 + PR)
                    act.wait_ge(o_ready, n * TI + t + 1)
                    nc.scalar.copy(o_raw[t % 2][:], o_acc[:]).then_inc(o_copied, 1)

                def item(pair, u, following, previous=True):
                    n = pair * 2 + u
                    for s, (t, j) in enumerate(units):
                        exponentials(n, s)
                        if s == 0 and following:
                            act.wait_ge(scores_made, n * U + 1)
                        for late in late_tile(n, s, previous):
                            copy_o(*late)
                        if following:
                            for p in range(TI):
                                for which in range(3):
                                    if SPLIT_SLOTS[p][which] == s:
                                        loads = ((n + 1) * (TI // 2) + p // 2 + 1) * 64
                                        split_copy(n + 1, 1 - u, p, which, loads)

                act.sem_inc(exp_done, 2)
                act.sem_inc(o_copied, 1)
                for p in range(TI):
                    for which in range(3):
                        split_copy(0, 0, p, which, (p // 2 + 1) * 64)
                item(0, 0, True, False)
                with act.Fori(0, PAIRS - 1) as pair:
                    item(pair, 1, True)
                    item(pair + 1, 0, True)
                item(PAIRS - 1, 1, False)
                copy_o(LAST_ITEM, TI - 1)

            @block.vector
            def _(dve):
                def reduce_chunk(m, k):
                    ib, c = chunks[k]
                    width = min(TILE, (ib + 1) * P - c * TILE)
                    for h in range(2):
                        dve.wait_ge(chunk_made, m * 2 * CH + 2 * k + h + 1)
                        nc.vector.tensor_reduce(part_max[:, h, ib, c:c + 1], rowwise[:, h, 0:width], AX.X,
                                                ALU.max).then_inc(chunk_reduced, 1)

                def finish_max(m):
                    dve.wait_ge(chunk_reduced, (m + 1) * 2 * CH)
                    nc.vector.tensor_reduce(neg_max[:, 0:2 * KB].rearrange("p (h b) -> p h b", h=2), part_max[:],
                                            AX.X, ALU.max, negate=True).then_inc(neg_max_ready, 1)

                def take_rows(m):
                    dve.wait_ge(max_turned, m + 1)
                    nc.vector.tensor_copy(max_rows[:], rowwise[:, 0, 0:P]).then_inc(max_rows_ready, 1)

                def add_unit(n, s):
                    t, j = units[s]
                    d = j - NB * t
                    off = d * P
                    dve.wait_ge(masked, n * DIAG + NB * t + d + 1)
                    if d == 0 and t == 0:
                        nc.vector.tensor_copy(sum_dve[t % 2][:], probs[s % PR][:]).then_inc(dve_added, 1)
                        return
                    if d == 0:
                        adds = sum(NB * q - 1 for q in range(1, t + 1))
                        dve.wait_ge(pool_added, n * POOL_ADDS + adds + 1)
                        nc.vector.tensor_tensor(sum_dve[t % 2][:], sum_pool[:], probs[s % PR][:],
                                                ALU.add).then_inc(dve_added, 1)
                        return
                    dve.wait_ge(dve_added, n * DIAG + NB * t + d + NB)
                    nc.vector.tensor_tensor(sum_dve[t % 2][:, :, off:], sum_dve[t % 2][:, :, off:], probs[s % PR][:, :, off:],
                                            ALU.add).then_inc(dve_added, 1)

                def reciprocals(n, t, part, parts):
                    if part == 0:
                        dve.wait_ge(denom_made, n * TI + t + 1)
                        dve.wait_ge(o_ready, n * TI + t + 2)
                    cols = slice(part * TILE // parts, (part + 1) * TILE // parts)
                    last = nc.vector.reciprocal(recip[:, cols], denom[:, cols])
                    if part == parts - 1:
                        last.then_inc(recip_ready, 1)

                def item(pair, u, following, previous=True):
                    n = pair * 2 + u
                    for s, (t, j) in enumerate(units):
                        if following:
                            for k in slot_chunks[s]:
                                reduce_chunk(n + 1, k)
                            if s == LAST_CHUNK_SLOT:
                                finish_max(n + 1)
                            if s == LAST_CHUNK_SLOT + 1:
                                take_rows(n + 1)
                        if j >= NB * t:
                            add_unit(n, s)
                        if following:
                            if K_DIFF_SLOTS[0] == s:
                                k_diff(dve, nc.vector, split_lo_k0, n + 1, 1 - u, 0)
                            for p in range(TI):
                                if Q_DIFF_SLOTS[p] == s:
                                    q_diff(dve, n + 1, 1 - u, p)
                        for part in range(RECIP_PARTS):
                            for late in late_tile(n, s - 2 - part, previous):
                                reciprocals(*late, part, RECIP_PARTS)

                dve.sem_inc(dve_added, NB)
                dve.sem_inc(recip_ready, 1)
                nc.vector.memset(part_max[:], LOWEST).then_inc(prepared, 1)
                nc.vector.memset(neg_max[:], 0.0).then_inc(prepared, 1)
                dve.wait_ge(prepared, 2)
                k_diff(dve, nc.vector, split_lo_k0, 0, 0, 0)
                q_diff(dve, 0, 0, 0)
                for p in range(TI):
                    mine = [k for k in range(CH) if chunks[k][0] // NB == p]
                    for k in mine:
                        if p + 1 < TI and k == mine[len(mine) // 2]:
                            q_diff(dve, 0, 0, p + 1)
                        ib, c = chunks[k]
                        width = min(TILE, (ib + 1) * P - c * TILE)
                        dve.wait_ge(chunk_made, 2 * k + 2)
                        nc.vector.tensor_reduce(part_max[:, :, ib, c], first_buffers[k % 3][:, :, 0:width], AX.X,
                                                ALU.max).then_inc(chunk_reduced, 2)
                finish_max(0)
                take_rows(0)
                item(0, 0, True, False)
                with dve.Fori(0, PAIRS - 1) as pair:
                    item(pair, 1, True)
                    item(pair + 1, 0, True)
                item(PAIRS - 1, 1, False)
                reciprocals(LAST_ITEM, TI - 1, 0, 1)

            @block.gpsimd
            def _(pool):
                def normalise(n, t):
                    pool.wait_ge(recip_ready, n * TI + t + 2)
                    pool.wait_ge(o_copied, n * TI + t + 2)
                    pool.wait_ge(o_stored, (n * TI + t) * 16 + 1)
                    nc.gpsimd.tensor_tensor(o_norm[:], o_raw[t % 2][:], recip[:], ALU.mult).then_inc(o_ready, 1)

                def item(pair, u, following, previous=True):
                    n = pair * 2 + u
                    adds = 0
                    for s, (t, j) in enumerate(units):
                        if j >= NB * t:
                            off = off_of(t, j)
                            wait_apart(pool, exp_done, n * U + s + 1 + 2, exp_done, 2)
                            block_ = probs[s % PR][:, :, off:off + P]
                            nc.gpsimd.affine_select(out=block_, in_=block_, compare_op=ALU.is_ge, fill=0.0, base=0,
                                                    pattern=[[0, 2], [1, P]], channel_multiplier=-1
                                                    ).then_inc(masked, 1)
                        elif j >= 1:
                            pool.wait_ge(exp_done, n * U + s + 1 + 2)
                            if j == 1:
                                pool.wait_ge(dve_added, n * DIAG + NB * (t - 1) + 1 + NB)
                                first = probs[(s - 1) % PR][:]
                            else:
                                pool.wait_ge(pool_added, n * POOL_ADDS + adds + 1)
                                first = sum_pool[:]
                            nc.gpsimd.tensor_tensor(sum_pool[:], first, probs[s % PR][:], ALU.add
                                                    ).then_inc(pool_added, 1)
                            adds += 1
                        for late in late_tile(n, s - 2 - RECIP_PARTS, previous):
                            normalise(*late)
                        if following:
                            for p in range(1, TI):
                                if K_DIFF_SLOTS[p] == s:
                                    k_diff(pool, nc.gpsimd, split_lo_k, n + 1, 1 - u, p)

                pool.sem_inc(pool_added, 1)
                pool.sem_inc(o_ready, 2)
                for u in range(2):
                    nc.gpsimd.memset(halves(k_l1[u][D:D + 1]), 1.0).then_inc(ones_placed, 1)
                pool.wait_ge(ones_placed, 2)
                for p in range(1, TI):
                    k_diff(pool, nc.gpsimd, split_lo_k, 0, 0, p)
                item(0, 0, True, False)
                with pool.Fori(0, PAIRS - 1) as pair:
                    item(pair, 1, True)
                    item(pair + 1, 0, True)
                item(PAIRS - 1, 1, False)
                normalise(LAST_ITEM, TI - 1)


def project_and_ffn(nc, x, o_t, bias, ffn_weights, out, consts):
    w_t, down_t, up_t, down_aux, up_aux_t = ffn_weights
    rank, udim = up_t.shape
    ddim = down_aux.shape[0]
    tokens, cin = x.shape
    hd = o_t.shape[0]
    KC = hd // P
    C = cin // P
    tiles = tokens // TILE
    ctx = ExitStack()
    with ctx:
        sb = lambda name, shape, dt=F32: ctx.enter_context(nc.sbuf_tensor("c_" + name, shape, dt))
        sem = lambda name: ctx.enter_context(nc.semaphore("c_" + name))
        w_in = sb("w_in", [P, C, cin])
        down = sb("down", [ddim, rank])
        aux = sb("aux", [ddim, cin])
        up = sb("up", [rank, udim])
        up_aux = sb("up_aux", [udim, cin])
        d_sb = sb("d_sb", [rank, cin])
        t_sb = sb("t_sb", [udim, cin])
        w_ffn_t = sb("w_ffn_t", [P, C, cin])
        wo_raw = consts["wo_raw"]
        wo_hi = sb("wo_hi", [P, KC, cin], F32R)
        wo_lo = sb("wo_lo", [P, KC, cin], F32R)
        bias_rows = sb("bias_rows", [P, cin])
        o_in = [sb(f"o_in{u}", [P, KC, TILE]) for u in range(2)]
        o_hi = [sb(f"o_hi{u}", [P, KC, TILE], F32R) for u in range(2)]
        o_lo = [sb(f"o_lo{u}", [P, KC, TILE], F32R) for u in range(2)]
        x_in = [sb(f"x_in{u}", [P, NB, cin]) for u in range(2)]
        x1 = [sb(f"x1{u}", [P, NB, cin]) for u in range(2)]
        x1b = [sb(f"x1b{u}", [P, NB, cin]) for u in range(2)]
        x_norm = [sb(f"x_norm{u}", [P, NB, cin]) for u in range(2)]
        out_sb = [sb(f"out_sb{u}", [P, NB, cin]) for u in range(2)]
        stats = [sb(f"stats{u}", [P, NB, 6]) for u in range(2)]
        mean_var = [sb(f"mean_var{u}", [P, NB, 2]) for u in range(2)]
        var_eps = [sb(f"var_eps{u}", [P, NB]) for u in range(2)]
        root = [sb(f"root{u}", [P, NB]) for u in range(2)]
        work = [sb(f"work{u}", [P, NB]) for u in range(2)]
        rstd = [sb(f"rstd{u}", [P, NB]) for u in range(2)]
        xt = [sb(f"xt{u}", [P, C, TILE]) for u in range(2)]
        y = [ctx.enter_context(nc.psum_tensor(f"c_y{u}", [P, NB, cin], F32)) for u in range(2)]
        turned = ctx.enter_context(nc.psum_tensor("c_turned", [P, C, TILE], F32))
        ffn = ctx.enter_context(nc.psum_tensor("c_ffn", [P, NB, cin], F32))
        l_ps, d_ps, t_ps = ffn[:, 0:C, :], ffn[0:rank, C, :], ffn[0:udim, C + 1, :]

        b_loaded = sem("b_loaded")
        merge_loaded = sem("merge_loaded")
        d_made = sem("d_made")
        d_copied = sem("d_copied")
        t_made = sem("t_made")
        t_copied = sem("t_copied")
        l_made = sem("l_made")
        merged = sem("merged")
        w_hi_ready = sem("w_hi_ready")
        w_lo_ready = sem("w_lo_ready")
        o_loaded = [sem(f"o_loaded{u}") for u in range(2)]
        x_loaded = [sem(f"x_loaded{u}") for u in range(2)]
        o_hi_ready = sem("o_hi_ready")
        o_lo_ready = sem("o_lo_ready")
        y_made = sem("y_made")
        x1_ready = sem("x1_ready")
        chain = sem("chain")
        var_ready = sem("var_ready")
        root_ready = sem("root_ready")
        normalised = sem("normalised")
        transposed = sem("transposed")
        xt_ready = sem("xt_ready")
        ffn_made = sem("ffn_made")
        biased = sem("biased")
        out_ready = sem("out_ready")
        stored = [sem(f"stored{u}") for u in range(2)]
        halfway = tiles // 2
        PARTS = 4
        first_loaded = [sem(f"first_loaded{p}") for p in range(PARTS)]

        with nc.Block() as block:

            @block.sync
            def _(sp):
                def load_o(T, u, ks, done):
                    sp.dma_start(o_in[u][:, ks, :], o_t[ks.start * P:ks.stop * P, bass.ds(T * TILE, TILE)].rearrange(
                        "(k p) t -> p k t", p=P)).then_inc(done, 16)

                def load_x(T, u):
                    sp.dma_start(x_in[u][:], x[bass.ds(T * TILE, TILE), :].rearrange("(n p) c -> p n c", p=P)
                                 ).then_inc(x_loaded[u], 16)

                def store(T, u):
                    wait_apart(sp, out_ready, T + 1 + 2, first_loaded[0], 16)
                    sp.dma_start(out[bass.ds(T * TILE, TILE), :].rearrange("(n p) c -> p n c", p=P), out_sb[u][:]
                                 ).then_inc(stored[u], 16)

                def step(T, u, ahead_o, ahead_x, store_last):
                    if ahead_o:
                        wait_apart(sp, o_lo_ready, T + 1 + PARTS, first_loaded[0], 16)
                        load_o(T + 3, 1 - u, slice(0, KC), o_loaded[1 - u])
                    if ahead_x:
                        wait_apart(sp, x1_ready, T + 1 + 2, first_loaded[0], 16)
                        load_x(T + 2, u)
                    if store_last:
                        store(T - 1, 1 - u)

                for u in range(2):
                    sp.sem_inc(stored[u], 1)
                for p in range(PARTS):
                    ks = slice(p * KC // PARTS, (p + 1) * KC // PARTS)
                    load_o(0, 0, ks, first_loaded[p])
                load_x(0, 0)
                load_o(1, 1, slice(0, KC), o_loaded[1])
                for dst, src in ((down[:], down_t[:, :]), (aux[:], down_aux[:, :]), (up[:], up_t[:, :]),
                                 (up_aux[:], up_aux_t[:, :]), (w_in[:], w_t.rearrange("(c p) n -> p c n", p=P))):
                    sp.dma_start(dst, src).then_inc(merge_loaded, 16)
                load_x(1, 1)
                sp.dma_start(bias_rows[:], bias.rearrange("(o n) -> o n", o=1).broadcast_to([P, cin])).then_inc(b_loaded, 16)
                sp.wait_ge(o_lo_ready, PARTS)
                load_o(2, 0, slice(0, KC), o_loaded[0])
                step(0, 0, True, True, False)
                with sp.Fori(0, halfway - 2) as i:
                    step(i * 2 + 1, 1, True, True, True)
                    step(i * 2 + 2, 0, True, True, True)
                step(tiles - 3, 1, False, True, True)
                step(tiles - 2, 0, False, False, True)
                store(tiles - 2, 0)
                store(tiles - 1, 1)
                for u in range(2):
                    sp.wait_ge(stored[u], 16 * halfway + 1)

            @block.tensor
            def _(pe):
                def out_project(T, u, blocks):
                    if blocks[0] == 0:
                        pe.wait_ge(o_lo_ready, T + PARTS)
                        pe.wait_ge(x1_ready, T + 1)
                    for n in blocks:
                        k = 0
                        for kc in range(KC):
                            for a, b in ((o_hi, wo_hi), (o_lo, wo_hi), (o_hi, wo_lo)):
                                last = nc.tensor.matmul(y[u][:, n, :], a[u][:, kc, n * P:(n + 1) * P], b[:, kc, :],
                                                        start=(k == 0), stop=(k == 3 * KC - 1))
                                k += 1
                    if blocks[-1] == NB - 1:
                        last.then_inc(y_made, 1)

                def transposes(T, u):
                    pe.wait_ge(normalised, T + 1)
                    for c in range(C):
                        for n in range(NB):
                            last = nc.tensor.transpose(turned[:, c, n * P:(n + 1) * P],
                                                       x_norm[u][:, n, c * P:(c + 1) * P], consts["ident"][:])
                    last.then_inc(transposed, 1)

                def feed_forward(T, u):
                    pe.wait_ge(merged, 1)
                    pe.wait_ge(xt_ready, T + 1)
                    pe.wait_ge(out_ready, T + 2)
                    for n in range(NB):
                        for c in range(C):
                            last = nc.tensor.matmul(ffn[:, n, :], xt[u][:, c, n * P:(n + 1) * P],
                                                    w_ffn_t[:, c, :], start=(c == 0), stop=(c == C - 1))
                    last.then_inc(ffn_made, 1)

                def step(T, u):
                    out_project(T, u, [0, 1])
                    transposes(T - 1, 1 - u)
                    out_project(T, u, [2, 3])
                    feed_forward(T - 1, 1 - u)

                pe.wait_ge(w_lo_ready, 1)
                out_project(0, 0, [0, 1, 2, 3])
                pe.wait_ge(merge_loaded, 16 * 5)
                nc.tensor.matmul(d_ps, down[:], aux[:], start=True, stop=True).then_inc(d_made, 1)
                pe.wait_ge(d_copied, 1)
                nc.tensor.matmul(t_ps, up[:], d_sb[:], start=True, stop=True).then_inc(t_made, 1)
                pe.wait_ge(t_copied, 1)
                for c in range(C):
                    last = nc.tensor.matmul(l_ps[:, c, :], t_sb[:, c * P:(c + 1) * P], up_aux[:], start=True, stop=True)
                last.then_inc(l_made, 1)
                with pe.Fori(0, halfway - 1) as i:
                    step(i * 2 + 1, 1)
                    step(i * 2 + 2, 0)
                step(tiles - 1, 1)
                transposes(tiles - 1, 1)
                feed_forward(tiles - 1, 1)

            @block.scalar
            def _(act):
                def high(T, u, loads):
                    act.wait_ge(o_loaded[u], (loads - (u == 0)) * 16)
                    act.wait_ge(y_made, T + 1)
                    nc.scalar.copy(o_hi[u][:], o_in[u][:]).then_inc(o_hi_ready, 1)

                def take_root(T, u):
                    act.wait_ge(var_ready, T + 1)
                    nc.scalar.activation(root[u][:], var_eps[u][:], ACT.Sqrt).then_inc(root_ready, 1)

                def turn(T, u):
                    act.wait_ge(transposed, T + 1)
                    nc.scalar.copy(xt[u][:], turned[:]).then_inc(xt_ready, 1)

                act.sem_inc(y_made, 2)
                nc.scalar.copy(wo_hi[:], wo_raw[:]).then_inc(w_hi_ready, 1)
                for p in range(PARTS):
                    ks = slice(p * KC // PARTS, (p + 1) * KC // PARTS)
                    act.wait_ge(first_loaded[p], 16)
                    nc.scalar.copy(o_hi[0][:, ks, :], o_in[0][:, ks, :]).then_inc(o_hi_ready, 1)
                high(1, 1, 1)
                take_root(0, 0)
                with act.Fori(0, halfway - 1) as i:
                    turn(i * 2, 0)
                    high(i * 2 + 2, 0, i + 2)
                    take_root(i * 2 + 1, 1)
                    turn(i * 2 + 1, 1)
                    high(i * 2 + 3, 1, i + 2)
                    take_root(i * 2 + 2, 0)
                turn(tiles - 2, 0)
                take_root(tiles - 1, 1)
                turn(tiles - 1, 1)

            @block.vector
            def _(dve):
                LINKS = 2 + ROOT_LINKS

                def low(T, u):
                    dve.wait_ge(o_hi_ready, T + PARTS)
                    nc.vector.tensor_tensor(o_lo[u][:], o_in[u][:], halves(o_hi[u][:]),
                                            ALU.subtract).then_inc(o_lo_ready, 1)

                def norm(T, u, loads):
                    dve.wait_ge(x_loaded[u], loads * 16)
                    dve.wait_ge(y_made, T + 1 + 2)
                    dve.wait_ge(biased, T + 1)
                    nc.vector.tensor_tensor(x1[u][:], y[u][:], x_in[u][:], ALU.add).then_inc(x1_ready, 1)
                    dve.wait_ge(x1_ready, T + 1 + 2)
                    for n in range(NB):
                        last = nc.vector.bn_stats(stats[u][:, n, :], x1[u][:, n, :])
                    last.then_inc(chain, 1)
                    wait_apart(dve, chain, T * LINKS + 1, x_loaded[0], 16)
                    for n in range(NB):
                        last = nc.vector.bn_aggr(mean_var[u][:, n, :], stats[u][:, n, :])
                    last.then_inc(chain, 1)
                    dve.wait_ge(chain, T * LINKS + 2)
                    nc.vector.tensor_scalar(var_eps[u][:], mean_var[u][:, :, 1], EPS, None,
                                            ALU.add).then_inc(var_ready, 1)
                    dve.wait_ge(root_ready, T + 1)
                    refined_rstd(nc, dve, chain, T * LINKS + 2, var_eps[u][:], root[u][:], rstd[u][:], work[u][:])
                    for n in range(NB):
                        last = nc.vector.tensor_scalar(x_norm[u][:, n, :], x1[u][:, n, :], mean_var[u][:, n, 0:1],
                                                       rstd[u][:, n:n + 1], ALU.subtract, ALU.mult)
                    last.then_inc(normalised, 1)

                def finish(T, u, uses):
                    dve.wait_ge(ffn_made, T + 1)
                    dve.wait_ge(biased, T + 1 + 2)
                    dve.wait_ge(stored[u], uses * 16 + 1)
                    nc.vector.tensor_tensor(out_sb[u][:], ffn[:], x1b[u][:], ALU.add).then_inc(out_ready, 1)

                dve.sem_inc(x1_ready, 2)
                dve.sem_inc(out_ready, 2)
                dve.wait_ge(w_hi_ready, 1)
                nc.vector.tensor_tensor(wo_lo[:], wo_raw[:], halves(wo_hi[:]), ALU.subtract).then_inc(w_lo_ready, 1)
                for p in range(PARTS):
                    ks = slice(p * KC // PARTS, (p + 1) * KC // PARTS)
                    dve.wait_ge(o_hi_ready, p + 1)
                    nc.vector.tensor_tensor(o_lo[0][:, ks, :], o_in[0][:, ks, :], halves(o_hi[0][:, ks, :]),
                                            ALU.subtract).then_inc(o_lo_ready, 1)
                low(1, 1)
                dve.wait_ge(d_made, 1)
                nc.vector.tensor_copy(d_sb[:], d_ps).then_inc(d_copied, 1)
                dve.wait_ge(t_made, 1)
                nc.vector.tensor_copy(t_sb[:], t_ps).then_inc(t_copied, 1)
                dve.wait_ge(l_made, 1)
                dve.wait_ge(merge_loaded, 16 * 5)
                nc.vector.tensor_tensor(w_ffn_t[:], l_ps, w_in[:], ALU.add).then_inc(merged, 1)
                norm(0, 0, 1)
                with dve.Fori(0, halfway - 1) as i:
                    low(i * 2 + 2, 0)
                    norm(i * 2 + 1, 1, i + 1)
                    finish(i * 2, 0, i)
                    low(i * 2 + 3, 1)
                    norm(i * 2 + 2, 0, i + 2)
                    finish(i * 2 + 1, 1, i)
                norm(tiles - 1, 1, halfway)
                finish(tiles - 2, 0, halfway - 1)
                finish(tiles - 1, 1, halfway - 1)

            @block.gpsimd
            def _(pool):
                pool.sem_inc(biased, 2)
                pool.wait_ge(b_loaded, 16)
                with pool.Fori(0, halfway) as i:
                    for u in range(2):
                        T = i * 2 + u
                        pool.wait_ge(x1_ready, T + 1 + 2)
                        pool.wait_ge(out_ready, T + 1)
                        for n in range(NB):
                            last = nc.gpsimd.tensor_tensor(x1b[u][:, n, :], x1[u][:, n, :], bias_rows[:], ALU.add)
                        last.then_inc(biased, 1)


def prepare(nc, consts):
    ctx = ExitStack()
    with ctx:
        filled = ctx.enter_context(nc.semaphore("p_filled"))

        with nc.Block() as block:

            @block.gpsimd
            def _(pool):
                nc.gpsimd.memset(consts["ident"][:], 0.0).then_inc(filled, 1)
                nc.gpsimd.memset(consts["ident_bf"][:], 0.0).then_inc(filled, 1)
                nc.gpsimd.memset(consts["above"][:], 0.0).then_inc(filled, 1)
                nc.gpsimd.memset(consts["ones"][:], 1.0).then_inc(filled, 1)
                pool.wait_ge(filled, 4)
                for name in ("ident", "ident_bf"):
                    nc.gpsimd.affine_select(out=consts[name][:], in_=consts[name][:], compare_op=ALU.not_equal,
                                            fill=1.0, base=0, pattern=[[-1, P]], channel_multiplier=1
                                            ).then_inc(filled, 1)
                nc.gpsimd.affine_select(out=consts["above"][:], in_=consts["above"][:], compare_op=ALU.is_ge,
                                        fill=LOWEST, base=0, pattern=[[-1, P]], channel_multiplier=1
                                        ).then_inc(filled, 1)
                pool.wait_ge(filled, 7)


def build(nc, x, w_qkv, w_out, w_t, bias, down_t, up_t, down_aux, up_aux_t, out):
    batches, length, cin = x.shape
    tokens = batches * length
    hd = w_qkv.shape[1] // 3
    rows = x.rearrange("b l c -> (b l) c")
    out_rows = out.rearrange("b l c -> (b l) c")
    q_t = nc.dram_tensor("q_t", [hd, tokens], F32).ap()
    k_t = nc.dram_tensor("k_t", [hd, tokens], F32).ap()
    v = nc.dram_tensor("v", [tokens, hd], F32).ap()
    o_t = nc.dram_tensor("o_t", [hd, tokens], F32).ap()
    with ExitStack() as ctx:
        sb = lambda name, shape, dt=F32: ctx.enter_context(nc.sbuf_tensor("p_" + name, shape, dt))
        consts = {
            "ident": sb("ident", [P, P]),
            "ident_bf": sb("ident_bf", [P, P], BF16),
            "above": sb("above", [P, P], BF16),
            "ones": sb("ones", [P, P]),
            "wo_raw": sb("wo_raw", [P, hd // P, cin]),
        }
        prepare(nc, consts)
        project_qkv(nc, rows, w_qkv, q_t, k_t, v, consts)
        attention(nc, q_t, k_t, v, o_t, w_out, batches, float(hd // HEADS) ** -0.5, consts)
        project_and_ffn(nc, rows, o_t, bias, (w_t, down_t, up_t, down_aux, up_aux_t), out_rows, consts)


def kernel(L0_attn_inputs, L0_attn_W_qkv, L0_attn_W_out, L0_ffn_W, L0_ffn_b, L0_ffn_lora_down,
           L0_ffn_lora_up, L0_ffn_down_aux, L0_ffn_up_aux):
    import numpy as np
    import concourse.bacc as bacc
    from concourse.bass_utils import run_bass_kernel_spmd

    given = {
        "x": L0_attn_inputs,
        "w_qkv": L0_attn_W_qkv,
        "w_out": L0_attn_W_out,
        "w_t": np.asarray(L0_ffn_W).T,
        "bias": L0_ffn_b,
        "down_t": np.asarray(L0_ffn_lora_down).T,
        "up_t": np.asarray(L0_ffn_lora_up).T,
        "down_aux": L0_ffn_down_aux,
        "up_aux_t": np.asarray(L0_ffn_up_aux).T,
    }
    nc = bacc.Bacc("TRN2", target_bir_lowering=False, num_devices=1)
    arrays, aps = {}, []
    for name, value in given.items():
        value = np.ascontiguousarray(value)
        arrays[f"in_{name}"] = value
        aps.append(nc.dram_tensor(f"in_{name}", value.shape, mybir.dt.from_np(value.dtype), kind="ExternalInput").ap())
    shape = arrays["in_x"].shape
    out = nc.dram_tensor("out", shape, F32, kind="ExternalOutput").ap()
    build(nc, *aps, out)
    result = run_bass_kernel_spmd(nc, [arrays], core_ids=[0])
    return result.results[0]["out"]
```
